# Optimizing a Trainium2 kernel written in Bass

```python
import numpy as np
import jax
import jax.numpy as jnp

def _softmax(x, axis=-1):
    return jax.nn.softmax(x, axis=axis)

def _gelu(x):
    return jax.nn.gelu(x, approximate=True)

def _silu(x):
    return jax.nn.silu(x)

def _sigmoid(x):
    return jax.nn.sigmoid(x)

def _layernorm(x, axis=-1, eps=1e-05):
    m = jnp.mean(x, axis=axis, keepdims=True)
    v = jnp.var(x, axis=axis, keepdims=True)
    return (x - m) / jnp.sqrt(v + eps)

def _scatter_add(tgt, idx, src, axis=0):
    return tgt.at[idx].add(src)

def _segment_sum(src, seg, n):
    return jax.ops.segment_sum(src, seg, n)
kernel_name = 'mk_adj_resnorm_d1_adj_r2_7b90ea'

def setup_inputs(seed: int=0):
    np.random.seed(seed)
    _w = jnp.asarray

    def _rec_inputs():
        import jax
        import jax.numpy as jnp
        _gk = jax.random.key(seed)
        x = -0.000929 + 1 * jax.random.normal(jax.random.fold_in(_gk, 1), (1354, 256), jnp.float32)
        _w = (1.0 + jnp.arange(1354, dtype=jnp.float32)) ** (-0.5)
        _w = _w / _w.mean()
        _pij = jnp.clip(0.0118168 * _w[:, None] * _w[None, :], 0.0, 1.0)
        _a = jax.random.uniform(jax.random.fold_in(_gk, 2), (1354, 1354)) < _pij
        _af = _a.astype(jnp.float32)
        _af = _af * jax.random.uniform(jax.random.fold_in(_gk, 3), (1354, 1354), jnp.float32, 0.05, 5.22011)
        adj = _af
        return (x, adj)
    x, adj = _rec_inputs()

    def _L0_gnn_setup():
        import jax, jax.numpy as jnp
        import numpy as np
        N = 1024
        HID = 256
        H = 8
        key = jax.random.key(seed)
        ks = jax.random.split(key, 8)
        x = jax.random.normal(ks[0], (N, HID), dtype=jnp.float32)
        sp = jax.random.normal(ks[1], (N, N), dtype=jnp.float32)
        zero_mask = jax.random.uniform(ks[2], (N, N)) < 0.2
        spatial_encoding = jnp.where(zero_mask, 0.0, sp)
        edge_encoding = jax.random.normal(ks[3], (N, N), dtype=jnp.float32)
        s = 1.0 / np.sqrt(HID)
        Wq = jax.random.normal(ks[4], (HID, HID * H), dtype=jnp.float32) * s
        Wk = jax.random.normal(ks[5], (HID, HID * H), dtype=jnp.float32) * s
        Wv = jax.random.normal(ks[6], (HID, HID * H), dtype=jnp.float32) * s
        Wout = jax.random.normal(ks[7], (HID * H, HID), dtype=jnp.float32) * (1.0 / np.sqrt(HID * H))
        return {'x': x, 'spatial_encoding': spatial_encoding, 'edge_encoding': edge_encoding, 'Wq': Wq, 'Wk': Wk, 'Wv': Wv, 'Wout': Wout}
    _L0_gnn_all = _L0_gnn_setup()
    _L0_gnn_in = {k: v for k, v in _L0_gnn_all.items() if k in ('Wq', 'Wk', 'Wv', 'Wout')}
    del _L0_gnn_all
    return {'x': x, 'adj': adj, 'L0_gnn_Wq': _L0_gnn_in['Wq'], 'L0_gnn_Wk': _L0_gnn_in['Wk'], 'L0_gnn_Wv': _L0_gnn_in['Wv'], 'L0_gnn_Wout': _L0_gnn_in['Wout']}

def reference(x, adj, L0_gnn_Wq, L0_gnn_Wk, L0_gnn_Wv, L0_gnn_Wout):
    import jax
    import jax.numpy as jnp

    def _L0_gnn_ref(x, spatial_encoding, edge_encoding, Wq, Wk, Wv, Wout):
        import jax, jax.numpy as jnp
        import numpy as np
        N = 1024
        HID = 256
        H = 8
        n, d = x.shape
        h = Wq.shape[1] // d
        scale = d ** (-0.5)
        q = (x @ Wq).reshape(h, n, d)
        k = (x @ Wk).reshape(h, n, d)
        v = (x @ Wv).reshape(h, n, d)
        a = jnp.einsum('hnd,hmd->hnm', q, k) * scale
        a = a + spatial_encoding + edge_encoding
        mask = spatial_encoding == 0.0
        a = jnp.where(mask, -1000000.0, a)
        a = jax.nn.softmax(a, axis=-1)
        a = jnp.where(mask, 0.0, a)
        out = jnp.einsum('hnm,hmd->hnd', a, v)
        out = out.transpose(1, 0, 2).reshape(n, h * d)
        return out @ Wout
    x = _layernorm(x + _L0_gnn_ref(x, adj, adj, L0_gnn_Wq, L0_gnn_Wk, L0_gnn_Wv, L0_gnn_Wout), axis=-1)
    return x

_drawn_inputs = setup_inputs


def setup_inputs(seed=0):
    import zlib

    import numpy as np

    out = dict(_drawn_inputs(seed))
    spreads = {}
    factors = {}
    for name, (base, spread) in spreads.items():
        noise = np.random.default_rng([zlib.crc32(name.encode()), seed]).standard_normal(out[name].shape)
        drawn = base * np.exp(spread * noise) if base else spread * noise
        out[name] = jnp.asarray(drawn.astype(out[name].dtype))
    for name, factor in factors.items():
        out[name] = (out[name] * factor).astype(out[name].dtype)
    return out
```

```python
import concourse.bass as bass
from concourse import mybir
from contextlib import ExitStack

FP32 = mybir.dt.float32
F32R = mybir.dt.float32r
ACT = mybir.ActivationFunctionType
ALU = mybir.AluOpType

N = 1354
D = 256
H = 8
P = 128
C = H
DC = D // P
TILES = -(-N // P)
NP = TILES * P
LAST = N - (TILES - 1) * P
WIN = N // C + 1
HALF = 4
NODES_HALF = HALF * N // C
PAD = 8
W1 = PAD + NP
BANK = 512
SETS = 3
GROUPS = 15
USES = GROUPS // SETS
TERMS = ((0, 0), (0, 1), (1, 0))
MASKED = 1e30
FLOOR = 1e6
NOFLOOR = 3e38
EPS = 1e-5


def program(nc, x, adj, wq, wk, wv, wout, y):
    kscr = nc.dram_tensor("k_spill", (H, P, DC, N), FP32, kind="Internal").ap()
    qscr = nc.dram_tensor("q_spill", (H, P, DC, NP), FP32, kind="Internal").ap()
    vscr = nc.dram_tensor("v_spill", (H, P, TILES * D), FP32, kind="Internal").ap()

    base = -(-nc.sbuf_base // 32) * 32

    class Region:
        at = base

        def __init__(self, size):
            size = -(-size // 32) * 32
            self.start, self.end = Region.at, Region.at + size
            Region.at = self.end
            self.next = self.start

        def put(self, name, shape, dt):
            size = 4
            for s in shape[1:]:
                size *= s
            size = -(-size // 32) * 32
            assert self.next + size <= self.end, name
            t = nc.alloc_sbuf_tensor_at(name, shape, dt, offset=self.next)
            self.next += size
            return t

        def again(self):
            self.next = self.start
            return self

    keep = Region(TILES * D * 4 + P * 4 + DC * D * 4 + 1280)
    acc = keep.put("acc", [P, TILES, D], FP32)
    ident = keep.put("ident", [P, P], FP32)
    zeros = keep.put("zeros", [P, DC, D], FP32)
    gate = keep.put("gate", [P, 1], FP32)
    nmin = keep.put("nmin", [P, 2], FP32)
    dsum = keep.put("dsum", [P, 2], FP32)
    eabs = keep.put("eabs", [P, 2], FP32)
    den = keep.put("den", [P, 2], FP32)
    rden = keep.put("rden", [P, 2], FP32)
    nabs = keep.put("nabs", [P, TILES], FP32)
    floor = keep.put("floor", [P, TILES], FP32)
    minus_floor = keep.put("minus_floor", [P, 1], FP32)
    eps = keep.put("eps", [P, 1], FP32)
    stats = keep.put("stats", [P, TILES, 6], FP32)
    mv = keep.put("mv", [P, TILES, 2], FP32)
    std = keep.put("std", [P, TILES], FP32)
    rstd = keep.put("rstd", [P, TILES], FP32)

    r = Region(4 * DC * C * D * 4)
    wk2 = [r.put(f"wk_{s}", [P, DC, C * D], F32R) for s in ("hi", "lo")]
    wq2 = [r.put(f"wq_{s}", [P, DC, C * D], F32R) for s in ("hi", "lo")]
    edge = r.again().put("edge", [P, TILES, N], FP32)
    r = Region(2 * DC * C * D * 4)
    wv2 = [r.put(f"wv_{s}", [P, DC, C * D], F32R) for s in ("hi", "lo")]
    r.again()
    k2 = [r.put(f"k_{s}", [P, DC, N], F32R) for s in ("hi", "lo")]
    q2 = [[r.put(f"q_{s}{b}", [P, DC, P], F32R) for s in ("hi", "lo")] for b in range(2)]
    r = Region(2 * DC * W1 * 4)
    vt2 = [r.put(f"vt_{s}", [P, DC, W1], F32R) for s in ("hi", "lo")]
    r.again()
    pt2 = [[r.put(f"pt_{s}{b}", [P, NP], F32R) for s in ("hi", "lo")] for b in range(2)]
    r = Region(2 * TILES * D * 4)
    xt2 = [r.put(f"xt_{s}", [P, DC, N], F32R) for s in ("hi", "lo")]
    r.again()
    v2 = [r.put(f"v_{s}", [P, TILES * D], F32R) for s in ("hi", "lo")]
    r = Region(4 * W1 * 4)
    kq_out = [r.put(f"kq_out{i}", [P, W1], FP32) for i in range(4)]
    r.again()
    prob = [r.put(f"prob{b}", [P, NP], FP32) for b in range(2)]
    qraw = r.put("qraw", [P, DC, NP], FP32)
    r = Region(2 * TILES * D * 4)
    land = [r.put(f"land{b}", [P, C * D], FP32) for b in range(2)]
    vp_out = r.again().put("vp_out", [P, TILES * D], FP32)
    vraw = r.again().put("vraw", [P, TILES * D], FP32)
    kraw = r.put("kraw", [P, DC, N], FP32)
    r = Region(3 * DC * D * 4)
    wo_raw = r.put("wo_raw", [P, DC, D], FP32)
    wo2 = [r.put(f"wo_{s}", [P, DC, D], F32R) for s in ("hi", "lo")]
    absent = r.again().put("absent", [P, N], FP32)

    with ExitStack() as ctx:
        ps = ctx.enter_context(nc.psum_tensor("ps", [P, 8 * BANK], FP32))
        sets = [ps[:, 2 * s * BANK:2 * (s + 1) * BANK].rearrange("p (c n) -> p c n", c=4) for s in range(SETS)]
        score = ps[:, 0:N]
        ptp = ps[:, 3 * BANK:3 * BANK + NP]
        pv = [ps[:, (6 + b) * BANK:(6 + b) * BANK + D] for b in range(2)]
        xtp = [ps[:, 0:N], ps[:, 3 * BANK:3 * BANK + N]]

        def sem(name):
            return ctx.enter_context(nc.semaphore(name))

        x_clear, x_loaded, ident_made, x_turned = sem("x_clear"), sem("x_loaded"), sem("ident_made"), sem("x_turned")
        xt_hi, xt_ready = sem("xt_hi"), sem("xt_ready")
        w_loaded = [sem(f"w_loaded{b}") for b in range(2)]
        wk_hi, wk_ready, w_hi, w_ready = sem("wk_hi"), sem("wk_ready"), sem("w_hi"), sem("w_ready")
        pads_clear = sem("pads_clear")
        wo_loaded, wo_hi, wo_ready = sem("wo_loaded"), sem("wo_hi"), sem("wo_ready")
        set_full = [sem(f"set_full{s}") for s in range(SETS)]
        set_free = [sem(f"set_free{s}") for s in range(SETS)]
        vt_hi = sem("vt_hi")
        kq_spilled = [sem(f"kq_spilled{i}") for i in range(4)]
        vp_spilled = sem("vp_spilled")
        adj_loaded = [sem(f"adj_loaded{b}") for b in range(TILES)]
        edge_clear, absent_known, edge_ready = sem("edge_clear"), sem("absent_known"), sem("edge_ready")
        no_absent, floor_ready = sem("no_absent"), sem("floor_ready")
        prob_clear, consts = sem("prob_clear"), sem("consts")
        zeros_made = sem("zeros_made")
        k_loaded, q_loaded, v_loaded = sem("k_loaded"), sem("q_loaded"), sem("v_loaded")
        k_hi, k_ready, v_hi, v_ready = sem("k_hi"), sem("k_ready"), sem("v_hi"), sem("v_ready")
        q_hi, q_ready = sem("q_hi"), sem("q_ready")
        scored, biased, exped, guarded = sem("scored"), sem("biased"), sem("exped"), sem("guarded")
        turned, pt_hi, pt_ready = sem("turned"), sem("pt_hi"), sem("pt_ready")
        summed, rden_ready, pv_done, added = sem("summed"), sem("rden_ready"), sem("pv_done"), sem("added")
        stat_done, mean_done, std_done, rstd_done, normed, stored = (
            sem("stat_done"), sem("mean_done"), sem("std_done"), sem("rstd_done"), sem("normed"), sem("stored"))

        RAISED = [*set_free, *set_full, wo_ready, scored, pv_done, added, pt_ready, biased]
        RAISED_BY_DMA = [*kq_spilled, vp_spilled]

        def after(n):
            return n + 1

        def after_dma(n):
            return n * 16 + 16

        def use(g, head):
            return head * USES + g // SETS

        def window(t, h4):
            return t[:, bass.ds(PAD - 2 * h4, WIN * C)].rearrange("p (i c) -> p i c", c=C)

        def tile_loop(eng, step):
            with eng.Fori(0, 4) as pair:
                for b in range(2):
                    step(pair * 2 + 1 + b, (1 + b) % 2)

        block = ctx.enter_context(nc.Block())

        @block.sync
        def _(sp):
            sp.dma_start(acc[:, 0:TILES - 1, :], x[0:(TILES - 1) * P, :].rearrange("(t p) d -> p t d", p=P)
                         ).then_inc(x_loaded, 16)
            sp.wait_ge(x_clear, 1)
            sp.dma_start(acc[0:LAST, TILES - 1, :], x[(TILES - 1) * P:N, :]).then_inc(x_loaded, 16)
            for n, (w, k) in enumerate((w, k) for w in (wk, wq, wv) for k in range(DC)):
                if 2 <= n < 4:
                    sp.wait_ge(wk_ready, n - 1)
                if n >= 4:
                    sp.wait_ge(w_ready, n - 3)
                sp.dma_start(land[n % 2][:, :], w[k * P:(k + 1) * P, :]).then_inc(w_loaded[n % 2], 16)
            with sp.Fori(0, 2) as hh:
                with sp.Fori(0, HALF) as h4:
                    head = hh * HALF + h4
                    sp.wait_ge(wo_ready, after(head))
                    sp.dma_start(wo_raw[:, :, :], wout[bass.ds(head * D, D), :].rearrange("(c p) n -> p c n", p=P)
                                 ).then_inc(wo_loaded, 16)
                    for i in range(4):
                        for g in (2 * i + 1, 2 * i):
                            sp.wait_ge(set_free[g % SETS], after(use(g, head) + 1))
                        if i < DC:
                            sp.dma_start(kscr[bass.ds(head, 1), :, i, :].rearrange("a p n -> (a p) n"),
                                         kq_out[i][:, PAD:PAD + N]).then_inc(kq_spilled[i], 16)
                        else:
                            sp.dma_start(qscr[bass.ds(head, 1), :, i - DC, :].rearrange("a p n -> (a p) n"),
                                         kq_out[i][:, PAD:PAD + NP]).then_inc(kq_spilled[i], 16)
                    for g in range(12, GROUPS):
                        sp.wait_ge(set_free[g % SETS], after(use(g, head) + 1))
                    sp.dma_start(vscr[bass.ds(head, 1)].rearrange("a p n -> (a p) n"), vp_out[:, :]
                                 ).then_inc(vp_spilled, 16)
            sp.wait_ge(wo_loaded, 16 * H)

            for i in range(4):
                sp.wait_ge(kq_spilled[i], after_dma(H))
            sp.dma_start(kraw[:, :, :], kscr[0]).then_inc(k_loaded, 16)
            sp.wait_ge(set_full[1], after(use(7, H - 1) + 1))
            for t in range(TILES - 1):
                sp.dma_start(edge[:, t, :], adj[t * P:(t + 1) * P, :]).then_inc(adj_loaded[t], 16)
                if t == 0:
                    sp.dma_start(qraw[:, :, :], qscr[0]).then_inc(q_loaded, 16)
                if t == 1:
                    sp.wait_ge(vp_spilled, after_dma(H))
                    sp.dma_start(vraw[:, :], vscr[0]).then_inc(v_loaded, 16)
            sp.wait_ge(edge_clear, 1)
            sp.dma_start(edge[0:LAST, TILES - 1, :], adj[(TILES - 1) * P:N, :]
                         ).then_inc(adj_loaded[TILES - 1], 16)
            with sp.Fori(1, H) as h:
                sp.wait_ge(k_ready, h * DC)
                sp.dma_start(kraw[:, :, :], kscr[bass.ds(h, 1)].rearrange("a p c n -> (a p) c n")
                             ).then_inc(k_loaded, 16)
                sp.wait_ge(v_ready, h)
                sp.dma_start(vraw[:, :], vscr[bass.ds(h, 1)].rearrange("a p n -> (a p) n")).then_inc(v_loaded, 16)
                sp.wait_ge(q_ready, h * TILES)
                sp.dma_start(qraw[:, :, :], qscr[bass.ds(h, 1)].rearrange("a p c n -> (a p) c n")
                             ).then_inc(q_loaded, 16)
            for t in range(TILES):
                rows = P if t < TILES - 1 else LAST
                sp.wait_ge(normed, t + 1)
                sp.dma_start(y[t * P:t * P + rows, :], acc[0:rows, t, :]).then_inc(stored, 16)
            sp.wait_ge(stored, 16 * TILES)

        @block.gpsimd
        def _(pool):
            for s in RAISED:
                pool.sem_inc(s, 1)
            for s in RAISED_BY_DMA:
                pool.sem_inc(s, 16)
            nc.gpsimd.memset(acc[:, TILES - 1, :], 0.0).then_inc(x_clear, 1)
            nc.gpsimd.memset(ident[:, :], 0.0).then_inc(ident_made, 1)
            pool.wait_ge(ident_made, 1)
            nc.gpsimd.affine_select(out=ident[:, :], in_=ident[:, :], compare_op=ALU.not_equal, fill=1.0, base=0,
                                    pattern=[[-1, P]], channel_multiplier=1).then_inc(ident_made, 1)
            nc.gpsimd.memset(zeros[:, :, :], 0.0).then_inc(zeros_made, 1)
            nc.gpsimd.memset(minus_floor[:, :], -FLOOR).then_inc(consts, 1)
            nc.gpsimd.memset(eps[:, :], EPS).then_inc(consts, 1)
            for t in kq_out:
                nc.gpsimd.memset(t[:, :], 0.0).then_inc(pads_clear, 1)
            for t in vt2:
                nc.gpsimd.memset(t[:, :, :].bitcast(FP32), 0.0).then_inc(pads_clear, 1)

            for n in range(2, 6):
                parts, k = (wq2, wq2, wv2, wv2)[n - 2], n % 2
                pool.wait_ge(w_loaded[n % 2], 16 * (n // 2 + 1))
                nc.gpsimd.tensor_copy(parts[0][:, k, :], land[n % 2][:, :]).then_inc(w_hi, 1)
                pool.wait_ge(w_hi, n - 1)
                nc.gpsimd.tensor_tensor(parts[1][:, k, :], land[n % 2][:, :], parts[0][:, k, :].bitcast(FP32),
                                        ALU.subtract).then_inc(w_ready, 1)

            pool.wait_ge(zeros_made, 1)
            with pool.Fori(0, H) as head:
                pool.wait_ge(wo_loaded, head * 16 + 16)
                pool.wait_ge(set_full[2], after(head * USES))
                nc.gpsimd.tensor_tensor(wo2[0][:, :, :], wo_raw[:, :, :], zeros[:, :, :], ALU.add).then_inc(wo_hi, 1)
                pool.wait_ge(wo_hi, head + 1)
                nc.gpsimd.tensor_tensor(wo2[1][:, :, :], wo_raw[:, :, :], wo2[0][:, :, :].bitcast(FP32),
                                        ALU.subtract).then_inc(wo_ready, 1)

            pool.wait_ge(set_full[1], after(use(7, H - 1) + 1))
            nc.gpsimd.memset(edge[:, TILES - 1, :], 0.0).then_inc(edge_clear, 1)
            for i in range(4):
                pool.wait_ge(kq_spilled[i], after_dma(H))
            for b in range(2):
                nc.gpsimd.memset(prob[b][:, N:NP], 0.0).then_inc(prob_clear, 1)

            pool.wait_ge(set_full[2], after(use(11, H - 1) + 1))
            with pool.Fori(0, H) as h:
                def stage(t, b):
                    src = qraw[:, :, t * P:(t + 1) * P]
                    nc.gpsimd.tensor_tensor(q2[b][0][:, :, :], src, zeros[:, :, 0:P], ALU.add).then_inc(q_hi, 1)
                    pool.wait_ge(q_hi, h * TILES + t + 1)
                    nc.gpsimd.tensor_tensor(q2[b][1][:, :, :], src, q2[b][0][:, :, :].bitcast(FP32),
                                            ALU.subtract).then_inc(q_ready, 1)

                pool.wait_ge(q_loaded, h * 16 + 16)
                pool.wait_ge(scored, after(h * TILES))
                for t in range(TILES):
                    if t >= 2:
                        pool.wait_ge(scored, after(h * TILES + t - 1))
                    stage(t, t % 2)

        @block.scalar
        def _(act):
            for k in range(DC):
                act.wait_ge(x_turned, k + 1)
                nc.scalar.activation(xt2[0][:, k, :], xtp[k], ACT.Copy).then_inc(xt_hi, 1)
            for k in range(DC):
                act.wait_ge(w_loaded[k], 16)
                nc.scalar.activation(wk2[0][:, k, :], land[k][:, :], ACT.Copy).then_inc(wk_hi, 1)

            act.wait_ge(pads_clear, 6)
            with act.Fori(0, 2) as hh:
                with act.Fori(0, HALF) as h4:
                    head = hh * HALF + h4
                    for g in range(12):
                        m, dc, cg = g // 4, g // 2 % 2, g % 2
                        src = sets[g % SETS][:, :, 0:WIN].rearrange("p c i -> p i c")
                        act.wait_ge(set_full[g % SETS], after(use(g, head) + 1))
                        if m < 2:
                            i = m * DC + dc
                            act.wait_ge(kq_spilled[i], after_dma(head))
                            nc.scalar.activation(window(kq_out[i], h4)[:, :, 4 * cg:4 * cg + 4], src, ACT.Copy,
                                                 scale=1.0 if m == 0 else -0.5 * D ** -0.5
                                                 ).then_inc(set_free[g % SETS], 1)
                        else:
                            nc.scalar.activation(window(vt2[0][:, dc, :], h4)[:, :, 4 * cg:4 * cg + 4], src,
                                                 ACT.Copy).then_inc(vt_hi, 1)

            act.wait_ge(consts, 2)
            act.wait_ge(set_full[2], after(use(11, H - 1) + 1))
            with act.Fori(0, H) as h:
                def turn(t, b, before):
                    act.wait_ge(turned, h * TILES + t + 1)
                    act.wait_ge(pv_done, after(before))
                    nc.scalar.activation(pt2[b][0][:, :], ptp, ACT.Copy).then_inc(pt_hi, 1)

                def exp(t, b):
                    act.wait_ge(biased, after(h * TILES + t + 1))
                    nc.scalar.activation(prob[b][:, 0:N], prob[b][:, 0:N], ACT.Exp, bias=nmin[:, b:b + 1],
                                         scale=-1.0, accum_out=dsum[:, b:b + 1]).then_inc(exped, 1)
                    nc.scalar.activation(eabs[:, b:b + 1], nmin[:, b:b + 1], ACT.Exp, bias=minus_floor[:, :]
                                         ).then_inc(guarded, 1)

                def step(t, b):
                    turn(t, b, h * TILES + t - 1)
                    exp(t + 1, 1 - b)

                act.wait_ge(k_loaded, h * 16 + 16)
                act.wait_ge(scored, after(h * TILES))
                for dc in range(DC):
                    nc.scalar.activation(k2[0][:, dc, :], kraw[:, dc, :], ACT.Copy).then_inc(k_hi, 1)
                act.wait_ge(v_loaded, h * 16 + 16)
                act.wait_ge(pv_done, after(h * TILES))
                nc.scalar.activation(v2[0][:, :], vraw[:, :], ACT.Copy).then_inc(v_hi, 1)
                exp(0, 0)
                turn(0, 0, h * TILES)
                exp(1, 1)
                turn(1, 1, h * TILES)
                exp(2, 0)
                turn(2, 0, h * TILES + 1)
                exp(3, 1)
                with act.Fori(1, 4) as pair:
                    step(pair * 2 + 1, 1)
                    step(pair * 2 + 2, 0)
                step(TILES - 2, 1)
                turn(TILES - 1, 0, h * TILES + TILES - 2)

            act.wait_ge(mean_done, TILES)
            nc.scalar.activation(std[:, :], mv[:, :, 1], ACT.Sqrt, bias=eps[:, :]).then_inc(std_done, 1)

        @block.vector
        def _(dve):
            for k in range(DC):
                dve.wait_ge(xt_hi, k + 1)
                nc.vector.tensor_tensor(xt2[1][:, k, :], xtp[k], xt2[0][:, k, :].bitcast(FP32), ALU.subtract
                                        ).then_inc(xt_ready, 1)
            for k in range(DC):
                dve.wait_ge(wk_hi, k + 1)
                nc.vector.tensor_tensor(wk2[1][:, k, :], land[k][:, :], wk2[0][:, k, :].bitcast(FP32),
                                        ALU.subtract).then_inc(wk_ready, 1)

            dve.wait_ge(pads_clear, 6)
            with dve.Fori(0, 2) as hh:
                with dve.Fori(0, HALF) as h4:
                    head = hh * HALF + h4
                    for g in range(8, 12):
                        dc, cg = g // 2 % 2, g % 2
                        src = sets[g % SETS][:, :, 0:WIN].rearrange("p c i -> p i c")
                        hi, lo = (window(v[:, dc, :], h4)[:, :, 4 * cg:4 * cg + 4] for v in vt2)
                        dve.wait_ge(vt_hi, head * 4 + g - 7)
                        nc.vector.tensor_tensor(lo, src, hi.bitcast(FP32), ALU.subtract
                                                ).then_inc(set_free[g % SETS], 1)
                    for g in range(12, GROUPS):
                        t0 = (g - 12) * 4
                        n = min(4, TILES - t0)
                        dve.wait_ge(set_full[g % SETS], after(use(g, head) + 1))
                        dve.wait_ge(vp_spilled, after_dma(head))
                        nc.vector.tensor_copy(vp_out[:, t0 * D:(t0 + n) * D].rearrange("p (c n) -> p c n", n=D),
                                              sets[g % SETS][:, 0:n, :]).then_inc(set_free[g % SETS], 1)

            dve.wait_ge(prob_clear, 2)

            def find_edges(t):
                dve.wait_ge(adj_loaded[t], 16)
                if t == TILES - 1:
                    dve.wait_ge(edge_clear, 1)
                if t:
                    dve.wait_ge(edge_ready, t)
                nc.vector.tensor_scalar(absent[:, :], edge[:, t, :], 0.0, 0.0, ALU.is_equal, ALU.add,
                                        accum_out=nabs[:, t:t + 1]).then_inc(absent_known, 1)
                dve.wait_ge(absent_known, t + 1)
                nc.vector.scalar_tensor_tensor(out=edge[:, t, :], in0=absent[:, :], scalar=MASKED / 2,
                                               in1=edge[:, t, :], op0=ALU.mult, op1=ALU.subtract
                                               ).then_inc(edge_ready, 1)
                nc.vector.tensor_scalar(floor[:, t:t + 1], nabs[:, t:t + 1], 0.0, NOFLOOR, ALU.is_equal, ALU.mult
                                        ).then_inc(no_absent, 1)
                dve.wait_ge(no_absent, t + 1)
                nc.vector.tensor_scalar(floor[:, t:t + 1], floor[:, t:t + 1], FLOOR, None, ALU.max
                                        ).then_inc(floor_ready, 1)
                dve.wait_ge(edge_ready, t + 1)

            def split_k(h):
                for dc in range(DC):
                    dve.wait_ge(k_hi, h * DC + dc + 1)
                    nc.vector.tensor_tensor(k2[1][:, dc, :], kraw[:, dc, :], k2[0][:, dc, :].bitcast(FP32),
                                            ALU.subtract).then_inc(k_ready, 1)

            def attend(h, first, last):
                def bias(t, b, before):
                    if first:
                        find_edges(t)
                    dve.wait_ge(scored, after(h * TILES + t + 1))
                    dve.wait_ge(turned, before)
                    nc.vector.memset(gate[:, :], 0.0)
                    dve.wait_ge(floor_ready, t + 1)
                    nc.vector.tensor_tensor_reduce(
                        out=prob[b][:, 0:N], in0=score, in1=edge[:, t, :], scale=2.0, scalar=floor[:, t:t + 1],
                        op0=ALU.add, op1=ALU.min, accum_out=nmin[:, b:b + 1]).then_inc(biased, 1)

                def low(t, b):
                    dve.wait_ge(pt_hi, h * TILES + t + 1)
                    nc.vector.tensor_tensor(pt2[b][1][:, :], ptp, pt2[b][0][:, :].bitcast(FP32), ALU.subtract
                                            ).then_inc(pt_ready, 1)
                    dve.wait_ge(exped, h * TILES + t + 1)
                    dve.wait_ge(guarded, h * TILES + t + 1)
                    nc.vector.scalar_tensor_tensor(out=den[:, b:b + 1], in0=eabs[:, b:b + 1], scalar=nabs[:, t:t + 1],
                                                   in1=dsum[:, b:b + 1], op0=ALU.mult, op1=ALU.add
                                                   ).then_inc(summed, 1)
                    dve.wait_ge(summed, h * TILES + t + 1)
                    nc.vector.reciprocal(rden[:, b:b + 1], den[:, b:b + 1]).then_inc(rden_ready, 1)

                def add(t, b):
                    dve.wait_ge(pv_done, after(h * TILES + t + 1))
                    dve.wait_ge(rden_ready, h * TILES + t + 1)
                    nc.vector.scalar_tensor_tensor(out=acc[:, t, :], in0=pv[b], scalar=rden[:, b:b + 1],
                                                   in1=acc[:, t, :], op0=ALU.mult, op1=ALU.add).then_inc(added, 1)

                def step(t, b):
                    bias(t + 1, 1 - b, h * TILES + t)
                    low(t, b)
                    add(t - 1, 1 - b)

                if first:
                    split_k(h)
                else:
                    dve.wait_ge(added, after(h * TILES))
                bias(0, 0, h * TILES)
                dve.wait_ge(v_hi, h + 1)
                nc.vector.tensor_tensor(v2[1][:, :], vraw[:, :], v2[0][:, :].bitcast(FP32), ALU.subtract
                                        ).then_inc(v_ready, 1)
                bias(1, 1, h * TILES)
                low(0, 0)
                for t in range(1, TILES - 1):
                    step(t, t % 2)
                low(TILES - 1, 0)
                if not last:
                    split_k(h + 1)
                add(TILES - 2, 1)
                add(TILES - 1, 0)

            attend(0, True, False)
            with dve.Fori(1, H - 1) as h:
                attend(h, False, False)
            attend(H - 1, False, True)

            dve.wait_ge(added, after(H * TILES))
            for t in range(TILES):
                nc.vector.bn_stats(stats[:, t, :], acc[:, t, :]).then_inc(stat_done, 1)
            for t in range(TILES):
                dve.wait_ge(stat_done, t + 1)
                nc.vector.bn_aggr(mv[:, t, :], stats[:, t, :]).then_inc(mean_done, 1)
            dve.wait_ge(std_done, 1)
            nc.vector.reciprocal(rstd[:, :], std[:, :]).then_inc(rstd_done, 1)
            dve.wait_ge(rstd_done, 1)
            for t in range(TILES):
                nc.vector.tensor_scalar(acc[:, t, :], acc[:, t, :], mv[:, t, 0:1], rstd[:, t:t + 1],
                                        ALU.subtract, ALU.mult).then_inc(normed, 1)

        @block.tensor
        def _(pe):
            pe.wait_ge(x_loaded, 32)
            pe.wait_ge(ident_made, 2)
            for k in range(DC):
                for t in range(TILES):
                    rows = P if t < TILES - 1 else LAST
                    last = nc.tensor.transpose(xtp[k][:, t * P:t * P + rows], acc[0:rows, t, k * P:(k + 1) * P],
                                               ident[0:rows, 0:rows])
                last.then_inc(x_turned, 1)
            pe.wait_ge(xt_ready, DC)

            with pe.Fori(0, 2) as hh:
                with pe.Fori(0, HALF) as h4:
                    head = hh * HALF + h4
                    for g in range(12):
                        m, dc, cg = g // 4, g // 2 % 2, g % 2
                        w2 = (wk2, wq2, wv2)[m]
                        if g == 0:
                            pe.wait_ge(wk_ready, DC)
                        if g == 4:
                            pe.wait_ge(w_ready, DC)
                        if g == 8:
                            pe.wait_ge(w_ready, 2 * DC)
                        pe.wait_ge(set_free[g % SETS], after(use(g, head)))
                        for c in range(4):
                            col = (4 * cg + c) * D + dc * P
                            for n, (k, (a, b)) in enumerate((k, ab) for k in range(DC) for ab in TERMS):
                                last = nc.tensor.matmul(
                                    sets[g % SETS][:, c, 0:WIN], w2[a][:, k, col:col + P],
                                    xt2[b][:, k, bass.ds(hh * NODES_HALF + h4 * (N // C), WIN)],
                                    start=n == 0, stop=n == 5)
                        last.then_inc(set_full[g % SETS], 1)
                    for g in (9, 10, 11):
                        pe.wait_ge(set_free[g % SETS], after(use(g, head) + 1))
                    pe.wait_ge(wo_ready, after(head + 1))
                    for g in range(12, GROUPS):
                        pe.wait_ge(set_free[g % SETS], after(use(g, head)))
                        for t in range((g - 12) * 4, min((g - 11) * 4, TILES)):
                            at = PAD + t * P
                            for n, (dc, (a, b)) in enumerate((dc, ab) for dc in range(DC) for ab in TERMS):
                                last = nc.tensor.matmul(sets[g % SETS][:, t % 4, :], vt2[a][:, dc, at:at + P],
                                                        wo2[b][:, dc, :], start=n == 0, stop=n == 5)
                        last.then_inc(set_full[g % SETS], 1)

            for s in range(SETS):
                pe.wait_ge(set_free[s], after(H * USES))
            with pe.Fori(0, H) as h:
                def scores(t, b):
                    pe.wait_ge(q_ready, h * TILES + t + 1)
                    pe.wait_ge(biased, after(h * TILES + t))
                    for n0 in range(0, N, BANK):
                        n1 = min(n0 + BANK, N)
                        for n, (dc, (i, j)) in enumerate((dc, ij) for dc in range(DC) for ij in TERMS):
                            last = nc.tensor.matmul(score[:, n0:n1], q2[b][i][:, dc, :], k2[j][:, dc, n0:n1],
                                                    start=n == 0, stop=n == 5)
                    last.then_inc(scored, 1)

                def turn(t, b):
                    pe.wait_ge(exped, h * TILES + t + 1)
                    pe.wait_ge(pt_ready, after(h * TILES + t))
                    for k in range(TILES):
                        last = nc.tensor.transpose(ptp[:, k * P:(k + 1) * P], prob[b][:, k * P:(k + 1) * P],
                                                   ident[:, :])
                    last.then_inc(turned, 1)

                def attend(t, b, before):
                    pe.wait_ge(pt_ready, after(h * TILES + t + 1))
                    pe.wait_ge(added, after(before))
                    for k in range(TILES):
                        for n, (i, j) in enumerate(TERMS):
                            last = nc.tensor.matmul(pv[b], pt2[b][i][:, k * P:(k + 1) * P],
                                                    v2[j][:, k * D:(k + 1) * D],
                                                    start=k == 0 and n == 0, stop=k == TILES - 1 and n == 2)
                    last.then_inc(pv_done, 1)

                def step(t, b):
                    scores(t + 1, 1 - b)
                    turn(t, b)
                    attend(t - 1, 1 - b, h * TILES + t - 2)

                pe.wait_ge(k_ready, h * DC + DC)
                scores(0, 0)
                scores(1, 1)
                turn(0, 0)
                scores(2, 0)
                turn(1, 1)
                pe.wait_ge(v_ready, h + 1)
                attend(0, 0, h * TILES)
                scores(3, 1)
                turn(2, 0)
                attend(1, 1, h * TILES)
                with pe.Fori(1, 4) as pair:
                    step(pair * 2 + 1, 1)
                    step(pair * 2 + 2, 0)
                step(TILES - 2, 1)
                turn(TILES - 1, 0)
                attend(TILES - 2, 1, h * TILES + TILES - 3)
                attend(TILES - 1, 0, h * TILES + TILES - 2)


def kernel(x, adj, L0_gnn_Wq, L0_gnn_Wk, L0_gnn_Wv, L0_gnn_Wout):
    import numpy as np
    import concourse.bacc as bacc
    from concourse.bass_utils import run_bass_kernel_spmd as run

    nc = bacc.Bacc("TRN2", target_bir_lowering=False, num_devices=1)
    arrays, args = {}, []
    for name, a in (("x", x), ("adj", adj), ("wq", L0_gnn_Wq), ("wk", L0_gnn_Wk), ("wv", L0_gnn_Wv),
                    ("wout", L0_gnn_Wout)):
        a = np.ascontiguousarray(a)
        arrays["in_" + name] = a
        args.append(nc.dram_tensor("in_" + name, a.shape, mybir.dt.from_np(a.dtype), kind="ExternalInput").ap())
    args.append(nc.dram_tensor("out_y", (N, D), FP32, kind="ExternalOutput").ap())
    program(nc, *args)
    return run(nc, [arrays], core_ids=[0]).results[0]["out_y"]
```

```python
import concourse.bass as bass
from concourse import mybir
from contextlib import ExitStack

FP32 = mybir.dt.float32
F32R = mybir.dt.float32r
ACT = mybir.ActivationFunctionType
ALU = mybir.AluOpType

N = 1354
D = 256
H = 8
P = 128
C = H
DC = D // P
TILES = -(-N // P)
NP = TILES * P
LAST = N - (TILES - 1) * P
PARTS = 3
STEP = (N - 1) // PARTS
WIN = STEP + 1
FLAT = N * C
BANK = 512
BUFS = 3
VGROUPS = ((0, 4), (4, 8), (8, TILES))
EARLY = 4
TERMS = ((0, 0), (0, 1), (1, 0))
MASKED = 1e30
FLOOR = 1e6
NOFLOOR = 3e38
EPS = 1e-5


def program(nc, x, adj, wq, wk, wv, wout, y):
    kscr, qscr, vscr = (nc.dram_tensor(f"{n}_spill", (P, DC, FLAT), FP32, kind="Internal").ap() for n in "kqv")

    base = -(-nc.sbuf_base // 32) * 32

    class Region:
        at = base

        def __init__(self, size):
            size = -(-size // 32) * 32
            self.start, self.end = Region.at, Region.at + size
            Region.at = self.end
            self.next = self.start

        def put(self, name, shape, dt):
            size = 4
            for s in shape[1:]:
                size *= s
            size = -(-size // 32) * 32
            assert self.next + size <= self.end, name
            t = nc.alloc_sbuf_tensor_at(name, shape, dt, offset=self.next)
            self.next += size
            return t

        def again(self):
            self.next = self.start
            return self

    keep = Region(TILES * D * 4 + P * 4 + DC * D * 4 + 1280)
    acc = keep.put("acc", [P, TILES, D], FP32)
    ident = keep.put("ident", [P, P], FP32)
    zeros = keep.put("zeros", [P, DC, D], FP32)
    gate = keep.put("gate", [P, 1], FP32)
    nmin = keep.put("nmin", [P, 2], FP32)
    dsum = keep.put("dsum", [P, 2], FP32)
    eabs = keep.put("eabs", [P, 2], FP32)
    den = keep.put("den", [P, 2], FP32)
    rden = keep.put("rden", [P, 2], FP32)
    nabs = keep.put("nabs", [P, TILES], FP32)
    floor = keep.put("floor", [P, TILES], FP32)
    minus_floor = keep.put("minus_floor", [P, 1], FP32)
    eps = keep.put("eps", [P, 1], FP32)
    stats = keep.put("stats", [P, TILES, 6], FP32)
    mv = keep.put("mv", [P, TILES, 2], FP32)
    std = keep.put("std", [P, TILES], FP32)
    rstd = keep.put("rstd", [P, TILES], FP32)

    r = Region(4 * DC * C * D * 4)
    wk2 = [r.put(f"wk_{s}", [P, DC, C * D], F32R) for s in ("hi", "lo")]
    wq2 = [r.put(f"wq_{s}", [P, DC, C * D], F32R) for s in ("hi", "lo")]
    r.again()
    edge = r.put("edge", [P, TILES, N], FP32)
    absent = r.put("absent", [P, N], FP32)
    r = Region(2 * DC * C * D * 4)
    wv2 = [r.put(f"wv_{s}", [P, DC, C * D], F32R) for s in ("hi", "lo")]
    r.again()
    k2 = [r.put(f"k_{s}", [P, DC, N], F32R) for s in ("hi", "lo")]
    q2 = [[r.put(f"q_{s}{b}", [P, DC, P], F32R) for s in ("hi", "lo")] for b in range(2)]
    wo_raw = r.put("wo_raw", [P, DC, D], FP32)
    wo2 = [r.put(f"wo_{s}", [P, DC, D], F32R) for s in ("hi", "lo")]
    r = Region(2 * TILES * D * 4)
    xt2 = [r.put(f"xt_{s}", [P, DC, N], F32R) for s in ("hi", "lo")]
    r.again()
    v2 = [r.put(f"v_{s}", [P, TILES * D], F32R) for s in ("hi", "lo")]
    r = Region(BUFS * WIN * C * 4)
    out_buf = [r.put(f"out_buf{i}", [P, WIN * C], FP32) for i in range(BUFS)]
    r.again()
    pt2 = [[r.put(f"pt_{s}{b}", [P, NP], F32R) for s in ("hi", "lo")] for b in range(2)]
    prob = [r.put(f"prob{b}", [P, NP], FP32) for b in range(2)]
    r.again()
    vt2 = [r.put(f"vt_{s}", [P, DC, NP], F32R) for s in ("hi", "lo")]
    r = Region(3 * DC * NP * 4)
    land = [r.put(f"land{b}", [P, C * D], FP32) for b in range(2)]
    r.again()
    kraw = r.put("kraw", [P, DC, N], FP32)
    qraw = r.put("qraw", [P, DC, NP], FP32)
    vraw = r.put("vraw", [P, DC, NP], FP32)

    with ExitStack() as ctx:
        ps = ctx.enter_context(nc.psum_tensor("ps", [P, 8 * BANK], FP32))
        sets = [ps[:, 4 * s * BANK:4 * (s + 1) * BANK].rearrange("p (c n) -> p c n", c=4) for s in range(2)]
        vps = [ps[:, b * BANK:(b + 2) * BANK].rearrange("p (c n) -> p c n", c=4) for b in (3, 5, 3)]
        score = ps[:, 0:N]
        ptp = ps[:, 3 * BANK:3 * BANK + NP]
        pv = [ps[:, (6 + b) * BANK:(6 + b) * BANK + D] for b in range(2)]
        xtp = [ps[:, 0:N], ps[:, 3 * BANK:3 * BANK + N]]

        def sem(name):
            return ctx.enter_context(nc.semaphore(name))

        x_clear, x_loaded, ident_made, x_turned = sem("x_clear"), sem("x_loaded"), sem("ident_made"), sem("x_turned")
        xt_hi, xt_ready = sem("xt_hi"), sem("xt_ready")
        w_loaded = [sem(f"w_loaded{b}") for b in range(2)]
        wk_hi, wk_ready, w_hi, w_ready = sem("wk_hi"), sem("wk_ready"), sem("w_hi"), sem("w_ready")
        pads_done = sem("pads_done")
        wo_loaded, wo_hi, wo_ready = sem("wo_loaded"), sem("wo_hi"), sem("wo_ready")
        set_full = [sem(f"set_full{s}") for s in range(2)]
        set_free = [sem(f"set_free{s}") for s in range(2)]
        spilled = [sem(f"spilled{i}") for i in range(BUFS)]
        vt_hi, vt_ready, vp_full = sem("vt_hi"), sem("vt_ready"), sem("vp_full")
        adj_loaded = [sem(f"adj_loaded{b}") for b in range(TILES)]
        edge_clear, absent_known, edge_ready = sem("edge_clear"), sem("absent_known"), sem("edge_ready")
        no_absent, floor_ready = sem("no_absent"), sem("floor_ready")
        prob_clear, consts = sem("prob_clear"), sem("consts")
        zeros_made = sem("zeros_made")
        k_loaded, q_loaded, v_loaded = sem("k_loaded"), sem("q_loaded"), sem("v_loaded")
        k_hi, k_ready, v_hi, v_ready = sem("k_hi"), sem("k_ready"), sem("v_hi"), sem("v_ready")
        q_hi, q_ready = sem("q_hi"), sem("q_ready")
        scored, biased, exped, guarded = sem("scored"), sem("biased"), sem("exped"), sem("guarded")
        turned, pt_hi, pt_ready = sem("turned"), sem("pt_hi"), sem("pt_ready")
        summed, rden_ready, pv_done, added = sem("summed"), sem("rden_ready"), sem("pv_done"), sem("added")
        stat_done, mean_done, std_done, rstd_done, normed, stored = (
            sem("stat_done"), sem("mean_done"), sem("std_done"), sem("rstd_done"), sem("normed"), sem("stored"))

        RAISED = [*set_free, wo_ready, vp_full, scored, pv_done, added, pt_ready, biased]
        RAISED_BY_DMA = spilled

        def after(n):
            return n + 1

        def after_dma(n):
            return n * 16 + 16

        def groups():
            for g in range(12):
                m, dc, cg = g // 4, g // 2 % 2, g % 2
                i = m * DC + dc
                yield m, dc, cg, g % 2, g // 2, i % BUFS, i // BUFS

        block = ctx.enter_context(nc.Block())

        @block.sync
        def _(sp):
            sp.dma_start(acc[:, 0:TILES - 1, :], x[0:(TILES - 1) * P, :].rearrange("(t p) d -> p t d", p=P)
                         ).then_inc(x_loaded, 16)
            sp.wait_ge(x_clear, 1)
            sp.dma_start(acc[0:LAST, TILES - 1, :], x[(TILES - 1) * P:N, :]).then_inc(x_loaded, 16)
            for n, (w, k) in enumerate((w, k) for w in (wk, wq, wv) for k in range(DC)):
                if 2 <= n < 4:
                    sp.wait_ge(wk_ready, n - 1)
                if n >= 4:
                    sp.wait_ge(w_ready, n - 3)
                sp.dma_start(land[n % 2][:, :], w[k * P:(k + 1) * P, :]).then_inc(w_loaded[n % 2], 16)
            with sp.Fori(0, PARTS - 1) as part:
                for m, dc, cg, s, u, buf, n in groups():
                    if cg == 1:
                        sp.wait_ge(set_free[s], after(part * 6 + u + 1))
                        sp.wait_ge(set_free[1 - s], after(part * 6 + u + 1))
                        sp.dma_start((kscr, qscr, vscr)[m][:, dc, bass.ds(part * (STEP * C), STEP * C)],
                                     out_buf[buf][:, 0:STEP * C]).then_inc(spilled[buf], 16)
            for m, dc, cg, s, u, buf, n in groups():
                if cg == 1:
                    sp.wait_ge(set_free[s], after((PARTS - 1) * 6 + u + 1))
                    sp.wait_ge(set_free[1 - s], after((PARTS - 1) * 6 + u + 1))
                    sp.dma_start((kscr, qscr, vscr)[m][:, dc, (PARTS - 1) * STEP * C:FLAT], out_buf[buf][:, :]
                                 ).then_inc(spilled[buf], 16)
                if (m, dc, cg) == (0, 1, 1):
                    sp.wait_ge(w_ready, 2 * DC)
                    for i in range(BUFS):
                        sp.wait_ge(spilled[i], after_dma(2))
                    sp.dma_start(kraw[:, :, :], kscr[:, :, 0:N]).then_inc(k_loaded, 16)
                    sp.wait_ge(pads_done, 2)
                    sp.dma_start(qraw[:, :, 0:N], qscr[:, :, 0:N]).then_inc(q_loaded, 16)
                    sp.dma_start(vraw[:, :, 0:N], vscr[:, :, 0:N]).then_inc(v_loaded, 16)
                if (m, dc, cg) == (1, 1, 1):
                    for s in range(2):
                        sp.wait_ge(set_full[s], (PARTS - 1) * 6 + 4)
                    for t in range(EARLY):
                        sp.dma_start(edge[:, t, :], adj[t * P:(t + 1) * P, :]).then_inc(adj_loaded[t], 16)
            for s in range(2):
                sp.wait_ge(set_full[s], PARTS * 6)
            sp.dma_start(wo_raw[:, :, :], wout[0:D, :].rearrange("(c p) n -> p c n", p=P)).then_inc(wo_loaded, 16)
            for t in range(EARLY, TILES - 1):
                sp.dma_start(edge[:, t, :], adj[t * P:(t + 1) * P, :]).then_inc(adj_loaded[t], 16)
            sp.wait_ge(edge_clear, 1)
            sp.dma_start(edge[0:LAST, TILES - 1, :], adj[(TILES - 1) * P:N, :]).then_inc(adj_loaded[TILES - 1], 16)
            for i in range(BUFS):
                sp.wait_ge(spilled[i], after_dma(PARTS * 2))
            with sp.Fori(1, H) as h:
                sp.wait_ge(k_ready, h * DC)
                sp.dma_start(kraw[:, :, :], kscr[:, :, bass.ds(h * N, N)]).then_inc(k_loaded, 16)
                sp.wait_ge(vt_ready, h * DC)
                sp.dma_start(vraw[:, :, 0:N], vscr[:, :, bass.ds(h * N, N)]).then_inc(v_loaded, 16)
                sp.wait_ge(wo_ready, after(h))
                sp.dma_start(wo_raw[:, :, :], wout[bass.ds(h * D, D), :].rearrange("(c p) n -> p c n", p=P)
                             ).then_inc(wo_loaded, 16)
                sp.wait_ge(q_ready, h * TILES)
                sp.dma_start(qraw[:, :, 0:N], qscr[:, :, bass.ds(h * N, N)]).then_inc(q_loaded, 16)
            for t in range(TILES):
                rows = P if t < TILES - 1 else LAST
                sp.wait_ge(normed, t + 1)
                sp.dma_start(y[t * P:t * P + rows, :], acc[0:rows, t, :]).then_inc(stored, 16)
            sp.wait_ge(stored, 16 * TILES)

        @block.gpsimd
        def _(pool):
            for s in RAISED:
                pool.sem_inc(s, 1)
            for s in RAISED_BY_DMA:
                pool.sem_inc(s, 16)
            nc.gpsimd.memset(acc[:, TILES - 1, :], 0.0).then_inc(x_clear, 1)
            nc.gpsimd.memset(ident[:, :], 0.0).then_inc(ident_made, 1)
            pool.wait_ge(ident_made, 1)
            nc.gpsimd.affine_select(out=ident[:, :], in_=ident[:, :], compare_op=ALU.not_equal, fill=1.0, base=0,
                                    pattern=[[-1, P]], channel_multiplier=1).then_inc(ident_made, 1)
            nc.gpsimd.memset(zeros[:, :, :], 0.0).then_inc(zeros_made, 1)
            nc.gpsimd.memset(minus_floor[:, :], -FLOOR).then_inc(consts, 1)
            nc.gpsimd.memset(eps[:, :], EPS).then_inc(consts, 1)

            for n in range(2, 6):
                parts, k = (wq2, wq2, wv2, wv2)[n - 2], n % 2
                pool.wait_ge(w_loaded[n % 2], 16 * (n // 2 + 1))
                nc.gpsimd.tensor_copy(parts[0][:, k, :], land[n % 2][:, :]).then_inc(w_hi, 1)
                pool.wait_ge(w_hi, n - 1)
                nc.gpsimd.tensor_tensor(parts[1][:, k, :], land[n % 2][:, :], parts[0][:, k, :].bitcast(FP32),
                                        ALU.subtract).then_inc(w_ready, 1)

            pool.wait_ge(w_ready, 2 * DC)
            for t in (qraw, vraw):
                nc.gpsimd.memset(t[:, :, N:NP], 0.0).then_inc(pads_done, 1)
            for s in range(2):
                pool.wait_ge(set_full[s], (PARTS - 1) * 6 + 4)
            nc.gpsimd.memset(edge[:, TILES - 1, :], 0.0).then_inc(edge_clear, 1)
            for i in range(BUFS):
                pool.wait_ge(spilled[i], after_dma(PARTS * 2))
            for b in range(2):
                nc.gpsimd.memset(prob[b][:, N:NP], 0.0).then_inc(prob_clear, 1)

            pool.wait_ge(zeros_made, 1)
            for s in range(2):
                pool.wait_ge(set_full[s], PARTS * 6)
            with pool.Fori(0, H) as h:
                def stage(t, b):
                    src = qraw[:, :, t * P:(t + 1) * P]
                    nc.gpsimd.tensor_tensor(q2[b][0][:, :, :], src, zeros[:, :, 0:P], ALU.add).then_inc(q_hi, 1)
                    pool.wait_ge(q_hi, h * TILES + t + 1)
                    nc.gpsimd.tensor_tensor(q2[b][1][:, :, :], src, q2[b][0][:, :, :].bitcast(FP32),
                                            ALU.subtract).then_inc(q_ready, 1)

                pool.wait_ge(wo_loaded, h * 16 + 16)
                pool.wait_ge(vp_full, after(h * len(VGROUPS)))
                nc.gpsimd.tensor_tensor(wo2[0][:, :, :], wo_raw[:, :, :], zeros[:, :, :], ALU.add).then_inc(wo_hi, 1)
                pool.wait_ge(wo_hi, h + 1)
                nc.gpsimd.tensor_tensor(wo2[1][:, :, :], wo_raw[:, :, :], wo2[0][:, :, :].bitcast(FP32),
                                        ALU.subtract).then_inc(wo_ready, 1)
                pool.wait_ge(q_loaded, h * 16 + 16)
                pool.wait_ge(scored, after(h * TILES))
                for t in range(TILES):
                    if t >= 2:
                        pool.wait_ge(scored, after(h * TILES + t - 1))
                    stage(t, t % 2)

        @block.scalar
        def _(act):
            for k in range(DC):
                act.wait_ge(x_turned, k + 1)
                nc.scalar.activation(xt2[0][:, k, :], xtp[k], ACT.Copy).then_inc(xt_hi, 1)
            for k in range(DC):
                act.wait_ge(w_loaded[k], 16)
                nc.scalar.activation(wk2[0][:, k, :], land[k][:, :], ACT.Copy).then_inc(wk_hi, 1)

            with act.Fori(0, PARTS) as part:
                for m, dc, cg, s, u, buf, n in groups():
                    act.wait_ge(set_full[s], part * 6 + u + 1)
                    act.wait_ge(spilled[buf], after_dma(part * 2 + n))
                    nc.scalar.activation(
                        out_buf[buf][:, :].rearrange("p (i c) -> p i c", c=C)[:, :, 4 * cg:4 * cg + 4],
                        sets[s][:, :, 0:WIN].rearrange("p c i -> p i c"), ACT.Copy,
                        scale=-0.5 * D ** -0.5 if m == 1 else 1.0).then_inc(set_free[s], 1)

            act.wait_ge(consts, 2)
            for s in range(2):
                act.wait_ge(set_full[s], PARTS * 6)
            for i in range(BUFS):
                act.wait_ge(spilled[i], after_dma(PARTS * 2))
            with act.Fori(0, H) as h:
                def turn(t, b, before):
                    act.wait_ge(turned, h * TILES + t + 1)
                    act.wait_ge(pv_done, after(before))
                    nc.scalar.activation(pt2[b][0][:, :], ptp, ACT.Copy).then_inc(pt_hi, 1)

                def exp(t, b):
                    act.wait_ge(biased, after(h * TILES + t + 1))
                    nc.scalar.activation(prob[b][:, 0:N], prob[b][:, 0:N], ACT.Exp, bias=nmin[:, b:b + 1],
                                         scale=-1.0, accum_out=dsum[:, b:b + 1]).then_inc(exped, 1)
                    nc.scalar.activation(eabs[:, b:b + 1], nmin[:, b:b + 1], ACT.Exp, bias=minus_floor[:, :]
                                         ).then_inc(guarded, 1)

                def step(t, b):
                    turn(t, b, h * TILES + t - 1)
                    exp(t + 1, 1 - b)

                act.wait_ge(k_loaded, h * 16 + 16)
                act.wait_ge(scored, after(h * TILES))
                for dc in range(DC):
                    nc.scalar.activation(k2[0][:, dc, :], kraw[:, dc, :], ACT.Copy).then_inc(k_hi, 1)
                act.wait_ge(v_loaded, h * 16 + 16)
                act.wait_ge(pv_done, after(h * TILES))
                for dc in range(DC):
                    nc.scalar.activation(vt2[0][:, dc, :], vraw[:, dc, :], ACT.Copy).then_inc(vt_hi, 1)
                exp(0, 0)
                for g, (t0, t1) in enumerate(VGROUPS):
                    act.wait_ge(vp_full, after(h * len(VGROUPS) + g + 1))
                    nc.scalar.activation(v2[0][:, t0 * D:t1 * D].rearrange("p (c n) -> p c n", n=D),
                                         vps[g][:, 0:t1 - t0, :], ACT.Copy).then_inc(v_hi, 1)
                exp(1, 1)
                turn(0, 0, h * TILES)
                exp(2, 0)
                turn(1, 1, h * TILES)
                turn(2, 0, h * TILES + 1)
                exp(3, 1)
                with act.Fori(1, 4) as pair:
                    step(pair * 2 + 1, 1)
                    step(pair * 2 + 2, 0)
                step(TILES - 2, 1)
                turn(TILES - 1, 0, h * TILES + TILES - 2)

            act.wait_ge(mean_done, TILES)
            nc.scalar.activation(std[:, :], mv[:, :, 1], ACT.Sqrt, bias=eps[:, :]).then_inc(std_done, 1)

        @block.vector
        def _(dve):
            for k in range(DC):
                dve.wait_ge(xt_hi, k + 1)
                nc.vector.tensor_tensor(xt2[1][:, k, :], xtp[k], xt2[0][:, k, :].bitcast(FP32), ALU.subtract
                                        ).then_inc(xt_ready, 1)
            for k in range(DC):
                dve.wait_ge(wk_hi, k + 1)
                nc.vector.tensor_tensor(wk2[1][:, k, :], land[k][:, :], wk2[0][:, k, :].bitcast(FP32),
                                        ALU.subtract).then_inc(wk_ready, 1)

            def find_edges(t):
                dve.wait_ge(adj_loaded[t], 16)
                if t == TILES - 1:
                    dve.wait_ge(edge_clear, 1)
                if t:
                    dve.wait_ge(edge_ready, t)
                nc.vector.tensor_scalar(absent[:, :], edge[:, t, :], 0.0, 0.0, ALU.is_equal, ALU.add,
                                        accum_out=nabs[:, t:t + 1]).then_inc(absent_known, 1)
                dve.wait_ge(absent_known, t + 1)
                nc.vector.scalar_tensor_tensor(out=edge[:, t, :], in0=absent[:, :], scalar=MASKED / 2,
                                               in1=edge[:, t, :], op0=ALU.mult, op1=ALU.subtract
                                               ).then_inc(edge_ready, 1)
                nc.vector.tensor_scalar(floor[:, t:t + 1], nabs[:, t:t + 1], 0.0, NOFLOOR, ALU.is_equal, ALU.mult
                                        ).then_inc(no_absent, 1)
                dve.wait_ge(no_absent, t + 1)
                nc.vector.tensor_scalar(floor[:, t:t + 1], floor[:, t:t + 1], FLOOR, None, ALU.max
                                        ).then_inc(floor_ready, 1)
                dve.wait_ge(edge_ready, t + 1)

            def split_k(h):
                for dc in range(DC):
                    dve.wait_ge(k_hi, h * DC + dc + 1)
                    nc.vector.tensor_tensor(k2[1][:, dc, :], kraw[:, dc, :], k2[0][:, dc, :].bitcast(FP32),
                                            ALU.subtract).then_inc(k_ready, 1)

            def attend(h, first, last):
                def bias(t, b, before):
                    if first and t >= EARLY:
                        find_edges(t)
                    dve.wait_ge(scored, after(h * TILES + t + 1))
                    dve.wait_ge(turned, before)
                    nc.vector.memset(gate[:, :], 0.0)
                    dve.wait_ge(floor_ready, t + 1)
                    nc.vector.tensor_tensor_reduce(
                        out=prob[b][:, 0:N], in0=score, in1=edge[:, t, :], scale=2.0, scalar=floor[:, t:t + 1],
                        op0=ALU.add, op1=ALU.min, accum_out=nmin[:, b:b + 1]).then_inc(biased, 1)

                def low(t, b):
                    dve.wait_ge(pt_hi, h * TILES + t + 1)
                    nc.vector.tensor_tensor(pt2[b][1][:, :], ptp, pt2[b][0][:, :].bitcast(FP32), ALU.subtract
                                            ).then_inc(pt_ready, 1)
                    dve.wait_ge(exped, h * TILES + t + 1)
                    dve.wait_ge(guarded, h * TILES + t + 1)
                    nc.vector.scalar_tensor_tensor(out=den[:, b:b + 1], in0=eabs[:, b:b + 1], scalar=nabs[:, t:t + 1],
                                                   in1=dsum[:, b:b + 1], op0=ALU.mult, op1=ALU.add
                                                   ).then_inc(summed, 1)
                    dve.wait_ge(summed, h * TILES + t + 1)
                    nc.vector.reciprocal(rden[:, b:b + 1], den[:, b:b + 1]).then_inc(rden_ready, 1)

                def add(t, b):
                    dve.wait_ge(pv_done, after(h * TILES + t + 1))
                    dve.wait_ge(rden_ready, h * TILES + t + 1)
                    nc.vector.scalar_tensor_tensor(out=acc[:, t, :], in0=pv[b], scalar=rden[:, b:b + 1],
                                                   in1=acc[:, t, :], op0=ALU.mult, op1=ALU.add).then_inc(added, 1)

                def step(t, b):
                    bias(t + 1, 1 - b, h * TILES + t)
                    low(t, b)
                    add(t - 1, 1 - b)

                if first:
                    split_k(h)
                else:
                    dve.wait_ge(added, after(h * TILES))
                for dc in range(DC):
                    dve.wait_ge(vt_hi, h * DC + dc + 1)
                    nc.vector.tensor_tensor(vt2[1][:, dc, :], vraw[:, dc, :], vt2[0][:, dc, :].bitcast(FP32),
                                            ALU.subtract).then_inc(vt_ready, 1)
                bias(0, 0, h * TILES)
                for g, (t0, t1) in enumerate(VGROUPS):
                    hi, lo = (v[:, t0 * D:t1 * D].rearrange("p (c n) -> p c n", n=D) for v in v2)
                    dve.wait_ge(v_hi, h * len(VGROUPS) + g + 1)
                    nc.vector.tensor_tensor(lo, vps[g][:, 0:t1 - t0, :], hi.bitcast(FP32), ALU.subtract
                                            ).then_inc(v_ready, 1)
                bias(1, 1, h * TILES)
                low(0, 0)
                for t in range(1, TILES - 1):
                    step(t, t % 2)
                low(TILES - 1, 0)
                if not last:
                    split_k(h + 1)
                add(TILES - 2, 1)
                add(TILES - 1, 0)

            for t in range(EARLY):
                find_edges(t)
            dve.wait_ge(prob_clear, 2)
            attend(0, True, False)
            with dve.Fori(1, H - 1) as h:
                attend(h, False, False)
            attend(H - 1, False, True)

            dve.wait_ge(added, after(H * TILES))
            for t in range(TILES):
                nc.vector.bn_stats(stats[:, t, :], acc[:, t, :]).then_inc(stat_done, 1)
            for t in range(TILES):
                dve.wait_ge(stat_done, t + 1)
                nc.vector.bn_aggr(mv[:, t, :], stats[:, t, :]).then_inc(mean_done, 1)
            dve.wait_ge(std_done, 1)
            nc.vector.reciprocal(rstd[:, :], std[:, :]).then_inc(rstd_done, 1)
            dve.wait_ge(rstd_done, 1)
            for t in range(TILES):
                nc.vector.tensor_scalar(acc[:, t, :], acc[:, t, :], mv[:, t, 0:1], rstd[:, t:t + 1],
                                        ALU.subtract, ALU.mult).then_inc(normed, 1)

        @block.tensor
        def _(pe):
            pe.wait_ge(x_loaded, 32)
            pe.wait_ge(ident_made, 2)
            for k in range(DC):
                for t in range(TILES):
                    rows = P if t < TILES - 1 else LAST
                    last = nc.tensor.transpose(xtp[k][:, t * P:t * P + rows], acc[0:rows, t, k * P:(k + 1) * P],
                                               ident[0:rows, 0:rows])
                last.then_inc(x_turned, 1)
            pe.wait_ge(xt_ready, DC)

            with pe.Fori(0, PARTS) as part:
                for m, dc, cg, s, u, buf, n in groups():
                    w2 = (wk2, wq2, wv2)[m]
                    if (dc, cg) == (0, 0):
                        pe.wait_ge(*((wk_ready, DC), (w_ready, DC), (w_ready, 2 * DC))[m])
                    pe.wait_ge(set_free[s], after(part * 6 + u))
                    for c in range(4):
                        col = (4 * cg + c) * D + dc * P
                        for n, (k, (a, b)) in enumerate((k, ab) for k in range(DC) for ab in TERMS):
                            last = nc.tensor.matmul(sets[s][:, c, 0:WIN], w2[a][:, k, col:col + P],
                                                    xt2[b][:, k, bass.ds(part * STEP, WIN)],
                                                    start=n == 0, stop=n == 5)
                    last.then_inc(set_full[s], 1)

            for s in range(2):
                pe.wait_ge(set_free[s], after(PARTS * 6))
            with pe.Fori(0, H) as h:
                def scores(t, b):
                    pe.wait_ge(q_ready, h * TILES + t + 1)
                    pe.wait_ge(biased, after(h * TILES + t))
                    for n0 in range(0, N, BANK):
                        n1 = min(n0 + BANK, N)
                        for n, (dc, (i, j)) in enumerate((dc, ij) for dc in range(DC) for ij in TERMS):
                            last = nc.tensor.matmul(score[:, n0:n1], q2[b][i][:, dc, :], k2[j][:, dc, n0:n1],
                                                    start=n == 0, stop=n == 5)
                    last.then_inc(scored, 1)

                def turn(t, b):
                    pe.wait_ge(exped, h * TILES + t + 1)
                    pe.wait_ge(pt_ready, after(h * TILES + t))
                    for k in range(TILES):
                        last = nc.tensor.transpose(ptp[:, k * P:(k + 1) * P], prob[b][:, k * P:(k + 1) * P],
                                                   ident[:, :])
                    last.then_inc(turned, 1)

                def attend(t, b, before):
                    pe.wait_ge(pt_ready, after(h * TILES + t + 1))
                    pe.wait_ge(added, after(before))
                    for k in range(TILES):
                        for n, (i, j) in enumerate(TERMS):
                            last = nc.tensor.matmul(pv[b], pt2[b][i][:, k * P:(k + 1) * P],
                                                    v2[j][:, k * D:(k + 1) * D],
                                                    start=k == 0 and n == 0, stop=k == TILES - 1 and n == 2)
                    last.then_inc(pv_done, 1)

                def step(t, b):
                    scores(t + 1, 1 - b)
                    turn(t, b)
                    attend(t - 1, 1 - b, h * TILES + t - 2)

                pe.wait_ge(k_ready, h * DC + DC)
                scores(0, 0)
                pe.wait_ge(vt_ready, h * DC + DC)
                pe.wait_ge(wo_ready, after(h + 1))
                pe.wait_ge(added, after(h * TILES))
                for g, (t0, t1) in enumerate(VGROUPS):
                    if g == 2:
                        pe.wait_ge(v_ready, h * len(VGROUPS) + 1)
                    for t in range(t0, t1):
                        for n, (dc, (a, b)) in enumerate((dc, ab) for dc in range(DC) for ab in TERMS):
                            last = nc.tensor.matmul(vps[g][:, t - t0, :], vt2[a][:, dc, t * P:(t + 1) * P],
                                                    wo2[b][:, dc, :], start=n == 0, stop=n == 5)
                    last.then_inc(vp_full, 1)
                scores(1, 1)
                pe.wait_ge(v_ready, (h + 1) * len(VGROUPS))
                turn(0, 0)
                scores(2, 0)
                turn(1, 1)
                attend(0, 0, h * TILES)
                scores(3, 1)
                turn(2, 0)
                attend(1, 1, h * TILES)
                with pe.Fori(1, 4) as pair:
                    step(pair * 2 + 1, 1)
                    step(pair * 2 + 2, 0)
                step(TILES - 2, 1)
                turn(TILES - 1, 0)
                attend(TILES - 2, 1, h * TILES + TILES - 3)
                attend(TILES - 1, 0, h * TILES + TILES - 2)


def kernel(x, adj, L0_gnn_Wq, L0_gnn_Wk, L0_gnn_Wv, L0_gnn_Wout):
    import numpy as np
    import concourse.bacc as bacc
    from concourse.bass_utils import run_bass_kernel_spmd as run

    nc = bacc.Bacc("TRN2", target_bir_lowering=False, num_devices=1)
    arrays, args = {}, []
    for name, a in (("x", x), ("adj", adj), ("wq", L0_gnn_Wq), ("wk", L0_gnn_Wk), ("wv", L0_gnn_Wv),
                    ("wout", L0_gnn_Wout)):
        a = np.ascontiguousarray(a)
        arrays["in_" + name] = a
        args.append(nc.dram_tensor("in_" + name, a.shape, mybir.dt.from_np(a.dtype), kind="ExternalInput").ap())
    args.append(nc.dram_tensor("out_y", (N, D), FP32, kind="ExternalOutput").ap())
    program(nc, *args)
    return run(nc, [arrays], core_ids=[0]).results[0]["out_y"]
```

```python
import concourse.bass as bass
from concourse import mybir
from contextlib import ExitStack

FP32 = mybir.dt.float32
F32R = mybir.dt.float32r
BF16 = mybir.dt.bfloat16
ACT = mybir.ActivationFunctionType
ALU = mybir.AluOpType

N = 1354
D = 256
H = 8
P = 128
C = H
DC = D // P
TILES = -(-N // P)
NP = TILES * P
LAST = N - (TILES - 1) * P
PARTS = 3
STEP = (N - 1) // PARTS
WIN = STEP + 1
FLAT = N * C
BANK = 512
CG = 4
GROUPS = 3 * DC * C // CG
USES = GROUPS // 2
EARLY_X = -(-WIN // P)
LANDS = 4
BUFS = 3
VGROUPS = ((0, 4), (4, 8), (8, TILES))
LAST_TILES = ((0, TILES - 2), (TILES - 2, TILES - 1), (TILES - 1, TILES))
EARLY = 2
TERMS = ((0, 0), (0, 1), (1, 0))
MASKED = 1e30
FLOOR = 1e6
NOFLOOR = 3e38
EPS = 1e-5


def program(nc, x, adj, wq, wk, wv, wout, y):
    kscr, qscr, vscr = (nc.dram_tensor(f"{n}_spill", (P, DC, FLAT), FP32, kind="Internal").ap() for n in "kqv")

    base = -(-nc.sbuf_base // 32) * 32

    class Region:
        at = base

        def __init__(self, size):
            size = -(-size // 32) * 32
            self.start, self.end = Region.at, Region.at + size
            Region.at = self.end
            self.next = self.start

        def put(self, name, shape, dt):
            size = 2 if dt == BF16 else 4
            for s in shape[1:]:
                size *= s
            size = -(-size // 32) * 32
            assert self.next + size <= self.end, name
            t = nc.alloc_sbuf_tensor_at(name, shape, dt, offset=self.next)
            self.next += size
            return t

        def again(self):
            self.next = self.start
            return self

    keep = Region(TILES * D * 4 + P * 4 + DC * D * 4 + 1280)
    acc = keep.put("acc", [P, TILES, D], FP32)
    ident = keep.put("ident", [P, P], FP32)
    zeros = keep.put("zeros", [P, DC, D], FP32)
    gate = keep.put("gate", [P, 1], FP32)
    nmin = keep.put("nmin", [P, 2], FP32)
    dsum = keep.put("dsum", [P, 2], FP32)
    eabs = keep.put("eabs", [P, 2], FP32)
    den = keep.put("den", [P, 2], FP32)
    rden = keep.put("rden", [P, 2], FP32)
    nabs = keep.put("nabs", [P, TILES], FP32)
    floor = keep.put("floor", [P, TILES], FP32)
    minus_floor = keep.put("minus_floor", [P, 1], FP32)
    eps = keep.put("eps", [P, 1], FP32)
    stats = keep.put("stats", [P, TILES, 6], FP32)
    mv = keep.put("mv", [P, TILES, 2], FP32)
    std = keep.put("std", [P, TILES], FP32)
    rstd = keep.put("rstd", [P, TILES], FP32)

    r = Region(4 * DC * C * D * 4)
    wk2 = [r.put(f"wk_{s}", [P, DC, C * D], F32R) for s in ("hi", "lo")]
    wv2 = [r.put(f"wv_{s}", [P, DC, C * D], F32R) for s in ("hi", "lo")]
    r.again()
    pt2 = [[r.put(f"pt_{s}{b}", [P, NP], F32R) for s in ("hi", "lo")] for b in range(2)]
    r.again()
    vt2 = [r.put(f"vt_{s}", [P, DC, NP], F32R) for s in ("hi", "lo")]
    k2 = [r.put(f"k_{s}", [P, DC, N], F32R) for s in ("hi", "lo")]
    q2 = [[r.put(f"q_{s}{b}", [P, DC, P], F32R) for s in ("hi", "lo")] for b in range(2)]
    wo_raw = r.put("wo_raw", [P, DC, D], FP32)
    wo2 = [r.put(f"wo_{s}", [P, DC, D], F32R) for s in ("hi", "lo")]
    edge = [r.put(f"edge{t}", [P, N], FP32) for t in range(EARLY)]
    r = Region(2 * DC * C * D * 4)
    wq2 = [r.put(f"wq_{s}", [P, DC, C * D], F32R) for s in ("hi", "lo")]
    r.again()
    edge += [r.put(f"edge{t}", [P, N], FP32) for t in range(EARLY, 7)]
    r = Region(2 * TILES * D * 4)
    xt2 = [r.put(f"xt_{s}", [P, DC, N], F32R) for s in ("hi", "lo")]
    r.again()
    v2 = r.put("v2", [P, TILES, 2, D], F32R)
    r = Region(WIN * C * 4)
    out_buf = [r.put("out_buf0", [P, WIN * C], FP32)]
    r.again()
    prob = [r.put(f"prob{b}", [P, NP], FP32) for b in range(2)]
    absent = r.put("absent", [P, N], BF16)
    r = Region((BUFS - 1) * WIN * C * 4)
    out_buf += [r.put(f"out_buf{i}", [P, WIN * C], FP32) for i in range(1, BUFS)]
    r.again()
    edge += [r.put(f"edge{t}", [P, N], FP32) for t in range(7, TILES)]
    r = Region(3 * DC * NP * 4)
    land = [r.put(f"land{b}", [P, C * D], FP32) for b in range(LANDS)]
    r.again()
    kraw = r.put("kraw", [P, DC, N], FP32)
    qraw = r.put("qraw", [P, DC, NP], FP32)
    vraw = r.put("vraw", [P, DC, NP], FP32)

    w2 = (wk2, wv2, wq2)

    with ExitStack() as ctx:
        ps = ctx.enter_context(nc.psum_tensor("ps", [P, 8 * BANK], FP32))
        sets = [ps[:, 4 * s * BANK:4 * (s + 1) * BANK].rearrange("p (c n) -> p c n", c=4) for s in range(2)]
        vps = [ps[:, b * BANK:(b + 2) * BANK].rearrange("p (c n) -> p c n", c=4) for b in (3, 5, 6)]
        score = ps[:, 0:N]
        ptp = ps[:, 3 * BANK:3 * BANK + NP]
        pv = [ps[:, (6 + b) * BANK:(7 + b) * BANK] for b in range(2)]
        xtp = [ps[:, 0:2 * BANK].rearrange("p (k n) -> p k n", k=DC)[:, :, 0:EARLY_X * P],
               ps[:, 4 * BANK:8 * BANK].rearrange("p (k n) -> p k n", k=DC)[:, :, 0:N - EARLY_X * P]]
        xt_nodes = ((0, EARLY_X * P), (EARLY_X * P, N))

        def sem(name):
            return ctx.enter_context(nc.semaphore(name))

        x_early, x_clear, x_loaded, ident_made, x_turned = (
            sem("x_early"), sem("x_clear"), sem("x_loaded"), sem("ident_made"), sem("x_turned"))
        xt_hi, xt_ready = sem("xt_hi"), sem("xt_ready")
        w_loaded = [sem(f"w_loaded{b}") for b in range(LANDS)]
        w_hi, w_ready = sem("w_hi"), sem("w_ready")
        pads_done = sem("pads_done")
        wo_loaded, wo_hi, wo_ready = sem("wo_loaded"), sem("wo_hi"), sem("wo_ready")
        set_full = [sem(f"set_full{s}") for s in range(2)]
        set_free = [sem(f"set_free{s}") for s in range(2)]
        spilled = [sem(f"spilled{i}") for i in range(BUFS)]
        vt_hi, vt_ready, vp_full = sem("vt_hi"), sem("vt_ready"), sem("vp_full")
        adj_loaded = [sem(f"adj_loaded{b}") for b in range(TILES)]
        edge_clear, absent_known, edge_ready = sem("edge_clear"), sem("absent_known"), sem("edge_ready")
        no_absent, floor_ready = sem("no_absent"), sem("floor_ready")
        prob_clear, consts = sem("prob_clear"), sem("consts")
        zeros_made = sem("zeros_made")
        k_loaded, q_loaded, v_loaded = sem("k_loaded"), sem("q_loaded"), sem("v_loaded")
        k_hi, k_ready, v_hi, v_ready = sem("k_hi"), sem("k_ready"), sem("v_hi"), sem("v_ready")
        q_hi, q_ready = sem("q_hi"), sem("q_ready")
        scored, biased, exped, guarded = sem("scored"), sem("biased"), sem("exped"), sem("guarded")
        turned, pt_hi, pt_ready = sem("turned"), sem("pt_hi"), sem("pt_ready")
        summed, rden_ready, pv_done, half_added, added = (
            sem("summed"), sem("rden_ready"), sem("pv_done"), sem("half_added"), sem("added"))
        stat_done, mean_done, std_done, rstd_done, normed, stored = (
            sem("stat_done"), sem("mean_done"), sem("std_done"), sem("rstd_done"), sem("normed"), sem("stored"))

        RAISED = [*set_free, wo_ready, vp_full, scored, pv_done, added, pt_ready, biased]
        RAISED_BY_DMA = spilled

        def after(n):
            return n + 1

        def after_dma(n):
            return n * 16 + 16

        def groups():
            for g in range(GROUPS):
                m, dc, cg = g // 4, g // 2 % 2, g % 2
                i = m * DC + dc
                yield m, dc, cg, g % 2, g // 2, i % BUFS, i // BUFS

        def pieces():
            half = C * D // 2
            cut = [(0, k, g * half, (g + 1) * half) for g in range(2) for k in range(DC)]
            cut += [(m, k, 0, C * D) for m in (1, 2) for k in range(DC)]
            for n, piece in enumerate(cut):
                yield *piece, n % LANDS, n // LANDS

        K_PIECES = 2 * DC
        PIECES = K_PIECES + 2 * DC

        block = ctx.enter_context(nc.Block())

        @block.sync
        def _(sp):
            sp.dma_start(acc[:, 0:EARLY_X, :], x[0:EARLY_X * P, :].rearrange("(t p) d -> p t d", p=P)
                         ).then_inc(x_early, 16)
            sp.dma_start(acc[:, EARLY_X:TILES - 1, :],
                         x[EARLY_X * P:(TILES - 1) * P, :].rearrange("(t p) d -> p t d", p=P)).then_inc(x_loaded, 16)
            sp.wait_ge(x_clear, 1)
            sp.dma_start(acc[0:LAST, TILES - 1, :], x[(TILES - 1) * P:N, :]).then_inc(x_loaded, 16)
            for n, (m, k, c0, c1, b, use) in enumerate(pieces()):
                if n >= LANDS:
                    sp.wait_ge(w_ready, n - LANDS + 1)
                sp.dma_start(land[b][:, c0:c1], (wk, wv, wq)[m][k * P:(k + 1) * P, c0:c1]).then_inc(w_loaded[b], 16)
            with sp.Fori(0, PARTS - 1) as part:
                for m, dc, cg, s, u, buf, n in groups():
                    if cg == 1:
                        sp.wait_ge(set_free[s], after(part * USES + u + 1))
                        sp.wait_ge(set_free[1 - s], after(part * USES + u + 1))
                        sp.dma_start((kscr, vscr, qscr)[m][:, dc, bass.ds(part * (STEP * C), STEP * C)],
                                     out_buf[buf][:, 0:STEP * C]).then_inc(spilled[buf], 16)
            sp.wait_ge(w_ready, PIECES)
            for i in range(BUFS):
                sp.wait_ge(spilled[i], after_dma(2))
            sp.dma_start(kraw[:, :, :], kscr[:, :, 0:N]).then_inc(k_loaded, 16)
            sp.wait_ge(pads_done, 2)
            sp.dma_start(qraw[:, :, 0:N], qscr[:, :, 0:N]).then_inc(q_loaded, 16)
            sp.dma_start(vraw[:, :, 0:N], vscr[:, :, 0:N]).then_inc(v_loaded, 16)
            for m, dc, cg, s, u, buf, n in groups():
                if cg == 1:
                    sp.wait_ge(set_free[s], after((PARTS - 1) * USES + u + 1))
                    sp.wait_ge(set_free[1 - s], after((PARTS - 1) * USES + u + 1))
                    sp.dma_start((kscr, vscr, qscr)[m][:, dc, (PARTS - 1) * STEP * C:FLAT], out_buf[buf][:, :]
                                 ).then_inc(spilled[buf], 16)
                if (m, dc, cg) == (1, 1, 1):
                    for s in range(2):
                        sp.wait_ge(set_full[s], (PARTS - 1) * USES + 2 * USES // 3)
                    sp.dma_start(wo_raw[:, :, :], wout[0:D, :].rearrange("(c p) n -> p c n", p=P)
                                 ).then_inc(wo_loaded, 16)
                    for t in range(EARLY):
                        sp.dma_start(edge[t][:, :], adj[t * P:(t + 1) * P, :]).then_inc(adj_loaded[t], 16)
            for s in range(2):
                sp.wait_ge(set_full[s], PARTS * USES)
            for t in range(EARLY, TILES - 1):
                if t == 7:
                    for i in range(BUFS):
                        sp.wait_ge(spilled[i], after_dma(PARTS * 2))
                sp.dma_start(edge[t][:, :], adj[t * P:(t + 1) * P, :]).then_inc(adj_loaded[t], 16)
            sp.wait_ge(edge_clear, 1)
            sp.dma_start(edge[TILES - 1][0:LAST, :], adj[(TILES - 1) * P:N, :]).then_inc(adj_loaded[TILES - 1], 16)
            with sp.Fori(1, H) as h:
                sp.wait_ge(k_ready, h * DC)
                sp.dma_start(kraw[:, :, :], kscr[:, :, bass.ds(h * N, N)]).then_inc(k_loaded, 16)
                sp.wait_ge(vt_ready, h * len(VGROUPS))
                sp.dma_start(vraw[:, :, 0:N], vscr[:, :, bass.ds(h * N, N)]).then_inc(v_loaded, 16)
                sp.wait_ge(wo_ready, after(h))
                sp.dma_start(wo_raw[:, :, :], wout[bass.ds(h * D, D), :].rearrange("(c p) n -> p c n", p=P)
                             ).then_inc(wo_loaded, 16)
                sp.wait_ge(q_ready, h * TILES)
                sp.dma_start(qraw[:, :, 0:N], qscr[:, :, bass.ds(h * N, N)]).then_inc(q_loaded, 16)
            for t in range(TILES):
                rows = P if t < TILES - 1 else LAST
                sp.wait_ge(normed, t + 1)
                sp.dma_start(y[t * P:t * P + rows, :], acc[0:rows, t, :]).then_inc(stored, 16)
            sp.wait_ge(stored, 16 * TILES)

        @block.gpsimd
        def _(pool):
            for s in RAISED:
                pool.sem_inc(s, 1)
            for s in RAISED_BY_DMA:
                pool.sem_inc(s, 16)
            nc.gpsimd.memset(acc[:, TILES - 1, :], 0.0).then_inc(x_clear, 1)
            nc.gpsimd.memset(ident[:, :], 0.0).then_inc(ident_made, 1)
            pool.wait_ge(ident_made, 1)
            nc.gpsimd.affine_select(out=ident[:, :], in_=ident[:, :], compare_op=ALU.not_equal, fill=1.0, base=0,
                                    pattern=[[-1, P]], channel_multiplier=1).then_inc(ident_made, 1)
            nc.gpsimd.memset(zeros[:, :, :], 0.0).then_inc(zeros_made, 1)
            nc.gpsimd.memset(minus_floor[:, :], -FLOOR).then_inc(consts, 1)
            nc.gpsimd.memset(eps[:, :], EPS).then_inc(consts, 1)

            pool.wait_ge(w_ready, PIECES)
            for t in (qraw, vraw):
                nc.gpsimd.memset(t[:, :, N:NP], 0.0).then_inc(pads_done, 1)
            pool.wait_ge(spilled[0], after_dma(PARTS * 2))
            for b in range(2):
                nc.gpsimd.memset(prob[b][:, N:NP], 0.0).then_inc(prob_clear, 1)

            pool.wait_ge(zeros_made, 1)
            for s in range(2):
                pool.wait_ge(set_full[s], (PARTS - 1) * USES + 2 * USES // 3)

            def attend(h, first):
                def stage(t, b):
                    src = qraw[:, :, t * P:(t + 1) * P]
                    nc.gpsimd.tensor_tensor(q2[b][0][:, :, :], src, zeros[:, :, 0:P], ALU.add).then_inc(q_hi, 1)
                    pool.wait_ge(q_hi, h * TILES + t + 1)
                    nc.gpsimd.tensor_tensor(q2[b][1][:, :, :], src, q2[b][0][:, :, :].bitcast(FP32),
                                            ALU.subtract).then_inc(q_ready, 1)

                pool.wait_ge(wo_loaded, h * 16 + 16)
                pool.wait_ge(vp_full, after(h * len(VGROUPS)))
                nc.gpsimd.tensor_tensor(wo2[0][:, :, :], wo_raw[:, :, :], zeros[:, :, :], ALU.add).then_inc(wo_hi, 1)
                pool.wait_ge(wo_hi, h + 1)
                nc.gpsimd.tensor_tensor(wo2[1][:, :, :], wo_raw[:, :, :], wo2[0][:, :, :].bitcast(FP32),
                                        ALU.subtract).then_inc(wo_ready, 1)
                pool.wait_ge(q_loaded, h * 16 + 16)
                pool.wait_ge(scored, after(h * TILES))
                for t in range(TILES):
                    if t >= 2:
                        pool.wait_ge(scored, after(h * TILES + t - 1))
                    stage(t, t % 2)
                    if first and t == 2:
                        for i in range(1, BUFS):
                            pool.wait_ge(spilled[i], after_dma(PARTS * 2))
                        nc.gpsimd.memset(edge[TILES - 1][:, :], 0.0).then_inc(edge_clear, 1)

            attend(0, True)
            with pool.Fori(1, H) as h:
                attend(h, False)

        @block.scalar
        def _(act):
            def split_x(i):
                n0, n1 = xt_nodes[i]
                act.wait_ge(x_turned, i + 1)
                nc.scalar.activation(xt2[0][:, :, n0:n1], xtp[i], ACT.Copy).then_inc(xt_hi, 1)

            split_x(0)
            for n, (m, k, c0, c1, b, use) in enumerate(pieces()):
                if m > 0:
                    break
                if n == DC:
                    split_x(1)
                act.wait_ge(w_loaded[b], 16 * use + 16)
                nc.scalar.activation(w2[m][0][:, k, c0:c1], land[b][:, c0:c1], ACT.Copy).then_inc(w_hi, 1)

            def unload(part, m, cg, s, u, buf, n):
                act.wait_ge(set_full[s], part * USES + u + 1)
                act.wait_ge(spilled[buf], after_dma(part * 2 + n))
                nc.scalar.activation(
                    out_buf[buf][:, :].rearrange("p (i c) -> p i c", c=C)[:, :, CG * cg:CG * cg + CG],
                    sets[s][:, :, 0:WIN].rearrange("p c i -> p i c"), ACT.Copy,
                    scale=-0.5 * D ** -0.5 if m == 2 else 1.0).then_inc(set_free[s], 1)

            def split_k(h):
                act.wait_ge(k_loaded, h * 16 + 16)
                act.wait_ge(scored, after(h * TILES))
                for dc in range(DC):
                    nc.scalar.activation(k2[0][:, dc, :], kraw[:, dc, :], ACT.Copy).then_inc(k_hi, 1)

            def split_v(h):
                act.wait_ge(v_loaded, h * 16 + 16)
                act.wait_ge(pv_done, after(h * TILES))
                for t0, t1 in VGROUPS:
                    nc.scalar.activation(vt2[0][:, :, t0 * P:t1 * P], vraw[:, :, t0 * P:t1 * P], ACT.Copy
                                         ).then_inc(vt_hi, 1)

            with act.Fori(0, PARTS - 1) as part:
                for m, dc, cg, s, u, buf, n in groups():
                    unload(part, m, cg, s, u, buf, n)
            for m, dc, cg, s, u, buf, n in groups():
                unload(PARTS - 1, m, cg, s, u, buf, n)
                if (m, dc, cg) == (1, 1, 1):
                    split_k(0)
                if (m, dc, cg) == (2, 0, 0):
                    split_v(0)

            act.wait_ge(consts, 2)

            def attend(h, first):
                def turn(t, b, before):
                    act.wait_ge(turned, h * TILES + t + 1)
                    act.wait_ge(pv_done, after(before))
                    nc.scalar.activation(pt2[b][0][:, :], ptp, ACT.Copy).then_inc(pt_hi, 1)

                def exp(t, b):
                    act.wait_ge(biased, after(h * TILES + t + 1))
                    nc.scalar.activation(prob[b][:, 0:N], prob[b][:, 0:N], ACT.Exp, bias=nmin[:, b:b + 1],
                                         scale=-1.0, accum_out=dsum[:, b:b + 1]).then_inc(exped, 1)
                    nc.scalar.activation(eabs[:, b:b + 1], nmin[:, b:b + 1], ACT.Exp, bias=minus_floor[:, :]
                                         ).then_inc(guarded, 1)

                def step(t, b):
                    turn(t, b, h * TILES + t - 1)
                    exp(t + 1, 1 - b)

                def split_vp(g):
                    t0, t1 = VGROUPS[g]
                    act.wait_ge(vp_full, after(h * len(VGROUPS) + g + 1))
                    nc.scalar.activation(v2[:, t0:t1, 0, :], vps[g][:, 0:t1 - t0, :], ACT.Copy).then_inc(v_hi, 1)

                if not first:
                    split_k(h)
                    split_v(h)
                exp(0, 0)
                split_vp(0)
                split_vp(1)
                exp(1, 1)
                turn(0, 0, h * TILES)
                turn(1, 1, h * TILES)
                exp(2, 0)
                turn(2, 0, h * TILES + 1)
                exp(3, 1)
                with act.Fori(1, 4) as pair:
                    step(pair * 2 + 1, 1)
                    step(pair * 2 + 2, 0)
                step(TILES - 2, 1)
                turn(TILES - 1, 0, h * TILES + TILES - 2)

            attend(0, True)
            with act.Fori(1, H) as h:
                attend(h, False)

            for t0, t1 in LAST_TILES:
                act.wait_ge(mean_done, t1)
                nc.scalar.activation(std[:, t0:t1], mv[:, t0:t1, 1], ACT.Sqrt, bias=eps[:, :]).then_inc(std_done, 1)

        @block.vector
        def _(dve):
            def split_x(i):
                n0, n1 = xt_nodes[i]
                dve.wait_ge(xt_hi, i + 1)
                nc.vector.tensor_tensor(xt2[1][:, :, n0:n1], xtp[i], xt2[0][:, :, n0:n1].bitcast(FP32), ALU.subtract
                                        ).then_inc(xt_ready, 1)

            split_x(0)
            for n, (m, k, c0, c1, b, use) in enumerate(pieces()):
                if n == DC:
                    split_x(1)
                if m > 0:
                    dve.wait_ge(w_loaded[b], 16 * use + 16)
                    nc.vector.tensor_copy(w2[m][0][:, k, c0:c1], land[b][:, c0:c1]).then_inc(w_hi, 1)
                dve.wait_ge(w_hi, n + 1)
                nc.vector.tensor_tensor(w2[m][1][:, k, c0:c1], land[b][:, c0:c1],
                                        w2[m][0][:, k, c0:c1].bitcast(FP32), ALU.subtract).then_inc(w_ready, 1)

            def find_edges(t):
                dve.wait_ge(adj_loaded[t], 16)
                if t == TILES - 1:
                    dve.wait_ge(edge_clear, 1)
                if t == 0:
                    dve.wait_ge(prob_clear, 2)
                else:
                    dve.wait_ge(edge_ready, t)
                nc.vector.tensor_scalar(absent[:, :], edge[t][:, :], 0.0, 0.0, ALU.is_equal, ALU.add,
                                        accum_out=nabs[:, t:t + 1]).then_inc(absent_known, 1)
                dve.wait_ge(absent_known, t + 1)
                nc.vector.scalar_tensor_tensor(out=edge[t][:, :], in0=absent[:, :], scalar=MASKED / 2,
                                               in1=edge[t][:, :], op0=ALU.mult, op1=ALU.subtract
                                               ).then_inc(edge_ready, 1)
                nc.vector.tensor_scalar(floor[:, t:t + 1], nabs[:, t:t + 1], 0.0, NOFLOOR, ALU.is_equal, ALU.mult
                                        ).then_inc(no_absent, 1)
                dve.wait_ge(no_absent, t + 1)
                nc.vector.tensor_scalar(floor[:, t:t + 1], floor[:, t:t + 1], FLOOR, None, ALU.max
                                        ).then_inc(floor_ready, 1)
                dve.wait_ge(edge_ready, t + 1)

            def split_k(h):
                for dc in range(DC):
                    dve.wait_ge(k_hi, h * DC + dc + 1)
                    nc.vector.tensor_tensor(k2[1][:, dc, :], kraw[:, dc, :], k2[0][:, dc, :].bitcast(FP32),
                                            ALU.subtract).then_inc(k_ready, 1)

            def attend(h, first, last):
                def bias(t, b, before):
                    if first and t >= EARLY:
                        find_edges(t)
                    dve.wait_ge(scored, after(h * TILES + t + 1))
                    dve.wait_ge(turned, before)
                    nc.vector.memset(gate[:, :], 0.0)
                    dve.wait_ge(floor_ready, t + 1)
                    nc.vector.tensor_tensor_reduce(
                        out=prob[b][:, 0:N], in0=score, in1=edge[t][:, :], scale=2.0, scalar=floor[:, t:t + 1],
                        op0=ALU.add, op1=ALU.min, accum_out=nmin[:, b:b + 1]).then_inc(biased, 1)

                def low(t, b):
                    dve.wait_ge(pt_hi, h * TILES + t + 1)
                    nc.vector.tensor_tensor(pt2[b][1][:, :], ptp, pt2[b][0][:, :].bitcast(FP32), ALU.subtract
                                            ).then_inc(pt_ready, 1)
                    dve.wait_ge(exped, h * TILES + t + 1)
                    dve.wait_ge(guarded, h * TILES + t + 1)
                    nc.vector.scalar_tensor_tensor(out=den[:, b:b + 1], in0=eabs[:, b:b + 1], scalar=nabs[:, t:t + 1],
                                                   in1=dsum[:, b:b + 1], op0=ALU.mult, op1=ALU.add
                                                   ).then_inc(summed, 1)
                    dve.wait_ge(summed, h * TILES + t + 1)
                    nc.vector.reciprocal(rden[:, b:b + 1], den[:, b:b + 1]).then_inc(rden_ready, 1)

                def add(t, b):
                    dve.wait_ge(pv_done, after(h * TILES + t + 1))
                    dve.wait_ge(rden_ready, h * TILES + t + 1)
                    rows = min(P, N - t * P)
                    for half, done in enumerate((half_added, added)):
                        if half == 1:
                            dve.wait_ge(half_added, h * TILES + t + 1)
                        nc.vector.scalar_tensor_tensor(
                            out=acc[0:rows, t, :], in0=pv[b][0:rows, half * D:(half + 1) * D],
                            scalar=rden[0:rows, b:b + 1], in1=acc[0:rows, t, :], op0=ALU.mult, op1=ALU.add
                        ).then_inc(done, 1)
                    if last:
                        dve.wait_ge(added, after(h * TILES + t + 1))
                        nc.vector.bn_stats(stats[:, t, :], acc[:, t, :]).then_inc(stat_done, 1)
                        dve.wait_ge(stat_done, t + 1)
                        nc.vector.bn_aggr(mv[:, t, :], stats[:, t, :]).then_inc(mean_done, 1)

                def normalise(n):
                    t0, t1 = LAST_TILES[n]
                    dve.wait_ge(std_done, n + 1)
                    nc.vector.reciprocal(rstd[:, t0:t1], std[:, t0:t1]).then_inc(rstd_done, 1)
                    dve.wait_ge(rstd_done, n + 1)
                    for t in range(t0, t1):
                        nc.vector.tensor_scalar(acc[:, t, :], acc[:, t, :], mv[:, t, 0:1], rstd[:, t:t + 1],
                                                ALU.subtract, ALU.mult).then_inc(normed, 1)

                def step(t, b):
                    bias(t + 1, 1 - b, h * TILES + t)
                    low(t, b)
                    add(t - 1, 1 - b)

                def split_vp(g):
                    t0, t1 = VGROUPS[g]
                    hi, lo = (v2[:, t0:t1, i, :] for i in range(2))
                    if g == 2:
                        dve.wait_ge(vp_full, after(h * len(VGROUPS) + g + 1))
                        nc.vector.tensor_copy(hi, vps[g][:, 0:t1 - t0, :]).then_inc(v_hi, 1)
                    dve.wait_ge(v_hi, h * len(VGROUPS) + g + 1)
                    nc.vector.tensor_tensor(lo, vps[g][:, 0:t1 - t0, :], hi.bitcast(FP32), ALU.subtract
                                            ).then_inc(v_ready, 1)

                if first:
                    split_k(h)
                else:
                    dve.wait_ge(added, after(h * TILES))
                for g, (t0, t1) in enumerate(VGROUPS):
                    hi, lo = (v[:, :, t0 * P:t1 * P] for v in vt2)
                    dve.wait_ge(vt_hi, h * len(VGROUPS) + g + 1)
                    nc.vector.tensor_tensor(lo, vraw[:, :, t0 * P:t1 * P], hi.bitcast(FP32), ALU.subtract
                                            ).then_inc(vt_ready, 1)
                if first:
                    for t in range(EARLY):
                        find_edges(t)
                bias(0, 0, h * TILES)
                split_vp(0)
                split_vp(1)
                bias(1, 1, h * TILES)
                split_vp(2)
                low(0, 0)
                for t in range(1, TILES - 1):
                    step(t, t % 2)
                low(TILES - 1, 0)
                if last:
                    normalise(0)
                else:
                    split_k(h + 1)
                add(TILES - 2, 1)
                add(TILES - 1, 0)
                if last:
                    normalise(1)
                    normalise(2)

            attend(0, True, False)
            with dve.Fori(1, H - 1) as h:
                attend(h, False, False)
            attend(H - 1, False, True)

        @block.tensor
        def _(pe):
            pe.wait_ge(ident_made, 2)
            for i, tiles in enumerate((range(EARLY_X), range(EARLY_X, TILES))):
                if i == 0:
                    pe.wait_ge(x_early, 16)
                else:
                    pe.wait_ge(x_loaded, 32)
                for k in range(DC):
                    for t in tiles:
                        rows, at = min(P, N - t * P), (t - tiles[0]) * P
                        last = nc.tensor.transpose(xtp[i][:, k, at:at + rows], acc[0:rows, t, k * P:(k + 1) * P],
                                                   ident[0:rows, 0:rows])
                last.then_inc(x_turned, 1)

            with pe.Fori(0, PARTS) as part:
                for m, dc, cg, s, u, buf, n in groups():
                    if (m, dc) == (0, 0):
                        pe.wait_ge(xt_ready, cg + 1)
                    pe.wait_ge(set_free[s], after(part * USES + u))
                    for k in range(DC):
                        if (m, dc) == (0, 0):
                            pe.wait_ge(w_ready, cg * DC + k + 1)
                        elif (dc, cg) == (0, 0):
                            pe.wait_ge(w_ready, K_PIECES + (m - 1) * DC + k + 1)
                        for c in range(CG):
                            col = (CG * cg + c) * D + dc * P
                            for n, (a, b) in enumerate(TERMS):
                                last = nc.tensor.matmul(sets[s][:, c, 0:WIN], w2[m][a][:, k, col:col + P],
                                                        xt2[b][:, k, bass.ds(part * STEP, WIN)],
                                                        start=k == 0 and n == 0, stop=k == DC - 1 and n == 2)
                    last.then_inc(set_full[s], 1)

            pe.wait_ge(set_free[0], after(PARTS * USES))
            with pe.Fori(0, H) as h:
                def scores(t, b):
                    pe.wait_ge(q_ready, h * TILES + t + 1)
                    pe.wait_ge(biased, after(h * TILES + t))
                    for n0 in range(0, N, BANK):
                        n1 = min(n0 + BANK, N)
                        for n, (dc, (i, j)) in enumerate((dc, ij) for dc in range(DC) for ij in TERMS):
                            last = nc.tensor.matmul(score[:, n0:n1], q2[b][i][:, dc, :], k2[j][:, dc, n0:n1],
                                                    start=n == 0, stop=n == 5)
                    last.then_inc(scored, 1)

                def turn(t, b, rows=P):
                    pe.wait_ge(exped, h * TILES + t + 1)
                    pe.wait_ge(pt_ready, after(h * TILES + t))
                    for k in range(TILES):
                        last = nc.tensor.transpose(ptp[:, k * P:k * P + rows], prob[b][0:rows, k * P:(k + 1) * P],
                                                   ident[0:rows, 0:rows])
                    last.then_inc(turned, 1)

                def attend(t, b, before, rows=P):
                    pe.wait_ge(pt_ready, after(h * TILES + t + 1))
                    pe.wait_ge(added, after(before))
                    for k in range(TILES):
                        hi, lo = (pt[:, k * P:k * P + rows] for pt in pt2[b])
                        nc.tensor.matmul(pv[b][0:rows, :], hi, v2[:, k, :, :].rearrange("p i n -> p (i n)"),
                                         start=k == 0, stop=False)
                        last = nc.tensor.matmul(pv[b][0:rows, 0:D], lo, v2[:, k, 0, :],
                                                start=False, stop=k == TILES - 1)
                    last.then_inc(pv_done, 1)

                def step(t, b):
                    scores(t + 1, 1 - b)
                    turn(t, b)
                    attend(t - 1, 1 - b, h * TILES + t - 2)

                pe.wait_ge(k_ready, h * DC + DC)
                scores(0, 0)
                pe.wait_ge(wo_ready, after(h + 1))
                pe.wait_ge(added, after(h * TILES))
                for g, (t0, t1) in enumerate(VGROUPS):
                    pe.wait_ge(vt_ready, h * len(VGROUPS) + g + 1)
                    if g == 0:
                        pe.wait_ge(set_free[1], after(PARTS * USES))
                    if g == 2:
                        scores(1, 1)
                        pe.wait_ge(v_ready, h * len(VGROUPS) + 2)
                    for t in range(t0, t1):
                        for n, (dc, (a, b)) in enumerate((dc, ab) for dc in range(DC) for ab in TERMS):
                            last = nc.tensor.matmul(vps[g][:, t - t0, :], vt2[a][:, dc, t * P:(t + 1) * P],
                                                    wo2[b][:, dc, :], start=n == 0, stop=n == 5)
                    last.then_inc(vp_full, 1)
                turn(0, 0)
                scores(2, 0)
                turn(1, 1)
                pe.wait_ge(v_ready, (h + 1) * len(VGROUPS))
                attend(0, 0, h * TILES)
                scores(3, 1)
                turn(2, 0)
                attend(1, 1, h * TILES)
                with pe.Fori(1, 4) as pair:
                    step(pair * 2 + 1, 1)
                    step(pair * 2 + 2, 0)
                step(TILES - 2, 1)
                turn(TILES - 1, 0, LAST)
                attend(TILES - 2, 1, h * TILES + TILES - 3)
                attend(TILES - 1, 0, h * TILES + TILES - 2, LAST)


def kernel(x, adj, L0_gnn_Wq, L0_gnn_Wk, L0_gnn_Wv, L0_gnn_Wout):
    import numpy as np
    import concourse.bacc as bacc
    from concourse.bass_utils import run_bass_kernel_spmd as run

    nc = bacc.Bacc("TRN2", target_bir_lowering=False, num_devices=1)
    arrays, args = {}, []
    for name, a in (("x", x), ("adj", adj), ("wq", L0_gnn_Wq), ("wk", L0_gnn_Wk), ("wv", L0_gnn_Wv),
                    ("wout", L0_gnn_Wout)):
        a = np.ascontiguousarray(a)
        arrays["in_" + name] = a
        args.append(nc.dram_tensor("in_" + name, a.shape, mybir.dt.from_np(a.dtype), kind="ExternalInput").ap())
    args.append(nc.dram_tensor("out_y", (N, D), FP32, kind="ExternalOutput").ap())
    program(nc, *args)
    return run(nc, [arrays], core_ids=[0]).results[0]["out_y"]
```
